# Optimizing a Trainium2 kernel written in Bass

```python
import numpy as np
import jax
import jax.numpy as jnp

def _softmax(x, axis=-1):
    return jax.nn.softmax(x, axis=axis)

def _gelu(x):
    return jax.nn.gelu(x, approximate=True)

def _silu(x):
    return jax.nn.silu(x)

def _sigmoid(x):
    return jax.nn.sigmoid(x)

def _layernorm(x, axis=-1, eps=1e-05):
    m = jnp.mean(x, axis=axis, keepdims=True)
    v = jnp.var(x, axis=axis, keepdims=True)
    return (x - m) / jnp.sqrt(v + eps)

def _scatter_add(tgt, idx, src, axis=0):
    return tgt.at[idx].add(src)

def _segment_sum(src, seg, n):
    return jax.ops.segment_sum(src, seg, n)
kernel_name = 'mk_xattn_seq_d2_seqx_r8_b43abb'

def setup_inputs(seed: int=0):
    np.random.seed(seed)
    _w = jnp.asarray

    def _rec_inputs():
        import jax
        import jax.numpy as jnp
        _rk = jax.random.key(seed)
        x = -0.0002928 + 1 * jax.random.normal(jax.random.fold_in(_rk, 1), (4, 256, 128), jnp.float32)
        _lenS = 256 - jax.random.randint(jax.random.fold_in(_rk, 7), (4,), 0, max(1, 256 // 4) + 1, jnp.int32)
        _lenS2 = 64 - jax.random.randint(jax.random.fold_in(_rk, 8), (4,), 0, max(1, 64 // 4) + 1, jnp.int32)
        _ctx_768P = jax.random.normal(jax.random.fold_in(_rk, 11), (4, 16, 96), jnp.float32)
        _ctx_768c = jax.random.dirichlet(jax.random.fold_in(_rk, 511), 0.3 * jnp.ones((16,), jnp.float32), (4, 64))
        _ctx_768t = jnp.einsum('bsk,bkd->bsd', _ctx_768c, _ctx_768P)
        _ctx_768t = _ctx_768t * jax.lax.rsqrt(jnp.mean(jnp.square(_ctx_768t)) + 1e-12) * 0.953939
        ctx_768 = 0.00095986 + 0.999812 * (_ctx_768t + 0.3 * jax.random.normal(jax.random.fold_in(_rk, 611), (4, 64, 96), jnp.float32))
        return (x, ctx_768)
    x, ctx_768 = _rec_inputs()

    def _L0_xattn_setup():
        import jax, jax.numpy as jnp
        import numpy as np
        B, S, L = (2, 256, 64)
        WIDTH, HEADS, CTX = (128, 16, 96)
        HD = WIDTH // HEADS
        EPS = 1e-05

        def _layernorm(x, g, b):
            m = jnp.mean(x, axis=-1, keepdims=True)
            v = jnp.mean(jnp.square(x - m), axis=-1, keepdims=True)
            return (x - m) * jax.lax.rsqrt(v + EPS) * g + b

        def _mha(q_in, kv_in, wq, bq, wk, bk, wv, bv, wo, bo):
            b = q_in.shape[0]
            q = (q_in @ wq.T + bq).reshape(b, -1, HEADS, HD).transpose(0, 2, 1, 3)
            k = (kv_in @ wk.T + bk).reshape(b, -1, HEADS, HD).transpose(0, 2, 1, 3)
            v = (kv_in @ wv.T + bv).reshape(b, -1, HEADS, HD).transpose(0, 2, 1, 3)
            scores = jnp.einsum('bhqd,bhkd->bhqk', q, k) * HD ** (-0.5)
            p = jax.nn.softmax(scores, axis=-1)
            o = jnp.einsum('bhqk,bhkd->bhqd', p, v)
            o = o.transpose(0, 2, 1, 3).reshape(b, -1, WIDTH)
            return o @ wo.T + bo
        key = jax.random.key(seed)
        ks = jax.random.split(key, 32)

        def xav(k, shape, gain=1.0):
            fan_out, fan_in = shape
            a = gain * np.sqrt(6.0 / (fan_in + fan_out))
            return jax.random.uniform(k, shape, jnp.float32, -a, a)
        g2 = 1.0 / np.sqrt(2.0)
        inp = {'x': jax.random.normal(ks[0], (B, S, WIDTH), jnp.float32), 'context': jax.random.normal(ks[1], (B, L, CTX), jnp.float32), 'ln1_g': jnp.ones((WIDTH,), jnp.float32), 'ln1_b': jnp.zeros((WIDTH,), jnp.float32), 'ln2_g': jnp.ones((WIDTH,), jnp.float32), 'ln2_b': jnp.zeros((WIDTH,), jnp.float32), 'ln3_g': jnp.ones((WIDTH,), jnp.float32), 'ln3_b': jnp.zeros((WIDTH,), jnp.float32), 'sa_wq': xav(ks[2], (WIDTH, WIDTH), g2), 'sa_bq': jnp.zeros((WIDTH,), jnp.float32), 'sa_wk': xav(ks[3], (WIDTH, WIDTH), g2), 'sa_bk': jnp.zeros((WIDTH,), jnp.float32), 'sa_wv': xav(ks[4], (WIDTH, WIDTH), g2), 'sa_bv': jnp.zeros((WIDTH,), jnp.float32), 'sa_wo': xav(ks[5], (WIDTH, WIDTH), 1.0), 'sa_bo': jnp.zeros((WIDTH,), jnp.float32), 'ca_wq': xav(ks[6], (WIDTH, WIDTH), g2), 'ca_bq': jnp.zeros((WIDTH,), jnp.float32), 'ca_wk': xav(ks[7], (WIDTH, CTX), g2), 'ca_bk': jnp.zeros((WIDTH,), jnp.float32), 'ca_wv': xav(ks[8], (WIDTH, CTX), g2), 'ca_bv': jnp.zeros((WIDTH,), jnp.float32), 'ca_wo': xav(ks[9], (WIDTH, WIDTH), 1.0), 'ca_bo': jnp.zeros((WIDTH,), jnp.float32), 'mlp_w1': 0.02 * jax.random.normal(ks[10], (4 * WIDTH, WIDTH), jnp.float32), 'mlp_b1': jnp.zeros((4 * WIDTH,), jnp.float32), 'mlp_w2': 0.02 * jax.random.normal(ks[11], (WIDTH, 4 * WIDTH), jnp.float32), 'mlp_b2': jnp.zeros((WIDTH,), jnp.float32)}
        return inp
    _L0_xattn_all = _L0_xattn_setup()
    _L0_xattn_in = {k: v for k, v in _L0_xattn_all.items() if k in ('ln1_g', 'ln1_b', 'ln2_g', 'ln2_b', 'ln3_g', 'ln3_b', 'sa_wq', 'sa_bq', 'sa_wk', 'sa_bk', 'sa_wv', 'sa_bv', 'sa_wo', 'sa_bo', 'ca_wq', 'ca_bq', 'ca_wk', 'ca_bk', 'ca_wv', 'ca_bv', 'ca_wo', 'ca_bo', 'mlp_w1', 'mlp_b1', 'mlp_w2', 'mlp_b2')}
    del _L0_xattn_all

    def _L1_xattn_setup():
        import jax, jax.numpy as jnp
        import numpy as np
        HEADS = 16
        D_HEAD = 64
        EPS = 1e-05

        def _ln(x, g, b):
            m = jnp.mean(x, axis=-1, keepdims=True)
            v = jnp.var(x, axis=-1, keepdims=True)
            return (x - m) * jax.lax.rsqrt(v + EPS) * g + b

        def _attn(xq, xc, Wq, Wk, Wv, Wo, bo):
            B, N, _ = xq.shape
            S = xc.shape[1]
            q = (xq @ Wq).reshape(B, N, HEADS, D_HEAD)
            k = (xc @ Wk).reshape(B, S, HEADS, D_HEAD)
            v = (xc @ Wv).reshape(B, S, HEADS, D_HEAD)
            scale = D_HEAD ** (-0.5)
            scores = jnp.einsum('bnhd,bshd->bhns', q, k) * scale
            attn = jax.nn.softmax(scores, axis=-1)
            out = jnp.einsum('bhns,bshd->bnhd', attn, v).reshape(B, N, HEADS * D_HEAD)
            return out @ Wo + bo

        def _geglu_ff(x, Wp, bp, Wf, bf):
            h = x @ Wp + bp
            a, gate = jnp.split(h, 2, axis=-1)
            return a * jax.nn.gelu(gate, approximate=False) @ Wf + bf
        key = jax.random.key(seed)
        ks = jax.random.split(key, 16)
        dim, ctx, inner, ffin = (128, 96, HEADS * D_HEAD, 4 * 128)

        def w(k, i, o):
            return jax.random.normal(k, (i, o), jnp.float32) * i ** (-0.5)
        inp = {'x': jax.random.normal(ks[0], (4, 256, dim), jnp.float32), 'context': jax.random.normal(ks[1], (4, 77, ctx), jnp.float32), 'Wq1': w(ks[2], dim, inner), 'Wk1': w(ks[3], dim, inner), 'Wv1': w(ks[4], dim, inner), 'Wo1': w(ks[5], inner, dim), 'bo1': jnp.zeros((dim,), jnp.float32), 'Wq2': w(ks[6], dim, inner), 'Wk2': w(ks[7], ctx, inner), 'Wv2': w(ks[8], ctx, inner), 'Wo2': w(ks[9], inner, dim), 'bo2': jnp.zeros((dim,), jnp.float32), 'Wp': w(ks[10], dim, 2 * ffin), 'bp': jnp.zeros((2 * ffin,), jnp.float32), 'Wf': w(ks[11], ffin, dim), 'bf': jnp.zeros((dim,), jnp.float32), 'g1': jnp.ones((dim,), jnp.float32), 'b1': jnp.zeros((dim,), jnp.float32), 'g2': jnp.ones((dim,), jnp.float32), 'b2': jnp.zeros((dim,), jnp.float32), 'g3': jnp.ones((dim,), jnp.float32), 'b3': jnp.zeros((dim,), jnp.float32)}
        return inp
    _L1_xattn_all = _L1_xattn_setup()
    _L1_xattn_in = {k: v for k, v in _L1_xattn_all.items() if k in ('Wq1', 'Wk1', 'Wv1', 'Wo1', 'bo1', 'Wq2', 'Wk2', 'Wv2', 'Wo2', 'bo2', 'Wp', 'bp', 'Wf', 'bf', 'g1', 'b1', 'g2', 'b2', 'g3', 'b3')}
    del _L1_xattn_all
    return {'x': x, 'ctx_768': ctx_768, 'L0_xattn_ln1_g': _L0_xattn_in['ln1_g'], 'L0_xattn_ln1_b': _L0_xattn_in['ln1_b'], 'L0_xattn_ln2_g': _L0_xattn_in['ln2_g'], 'L0_xattn_ln2_b': _L0_xattn_in['ln2_b'], 'L0_xattn_ln3_g': _L0_xattn_in['ln3_g'], 'L0_xattn_ln3_b': _L0_xattn_in['ln3_b'], 'L0_xattn_sa_wq': _L0_xattn_in['sa_wq'], 'L0_xattn_sa_bq': _L0_xattn_in['sa_bq'], 'L0_xattn_sa_wk': _L0_xattn_in['sa_wk'], 'L0_xattn_sa_bk': _L0_xattn_in['sa_bk'], 'L0_xattn_sa_wv': _L0_xattn_in['sa_wv'], 'L0_xattn_sa_bv': _L0_xattn_in['sa_bv'], 'L0_xattn_sa_wo': _L0_xattn_in['sa_wo'], 'L0_xattn_sa_bo': _L0_xattn_in['sa_bo'], 'L0_xattn_ca_wq': _L0_xattn_in['ca_wq'], 'L0_xattn_ca_bq': _L0_xattn_in['ca_bq'], 'L0_xattn_ca_wk': _L0_xattn_in['ca_wk'], 'L0_xattn_ca_bk': _L0_xattn_in['ca_bk'], 'L0_xattn_ca_wv': _L0_xattn_in['ca_wv'], 'L0_xattn_ca_bv': _L0_xattn_in['ca_bv'], 'L0_xattn_ca_wo': _L0_xattn_in['ca_wo'], 'L0_xattn_ca_bo': _L0_xattn_in['ca_bo'], 'L0_xattn_mlp_w1': _L0_xattn_in['mlp_w1'], 'L0_xattn_mlp_b1': _L0_xattn_in['mlp_b1'], 'L0_xattn_mlp_w2': _L0_xattn_in['mlp_w2'], 'L0_xattn_mlp_b2': _L0_xattn_in['mlp_b2'], 'L1_xattn_Wq1': _L1_xattn_in['Wq1'], 'L1_xattn_Wk1': _L1_xattn_in['Wk1'], 'L1_xattn_Wv1': _L1_xattn_in['Wv1'], 'L1_xattn_Wo1': _L1_xattn_in['Wo1'], 'L1_xattn_bo1': _L1_xattn_in['bo1'], 'L1_xattn_Wq2': _L1_xattn_in['Wq2'], 'L1_xattn_Wk2': _L1_xattn_in['Wk2'], 'L1_xattn_Wv2': _L1_xattn_in['Wv2'], 'L1_xattn_Wo2': _L1_xattn_in['Wo2'], 'L1_xattn_bo2': _L1_xattn_in['bo2'], 'L1_xattn_Wp': _L1_xattn_in['Wp'], 'L1_xattn_bp': _L1_xattn_in['bp'], 'L1_xattn_Wf': _L1_xattn_in['Wf'], 'L1_xattn_bf': _L1_xattn_in['bf'], 'L1_xattn_g1': _L1_xattn_in['g1'], 'L1_xattn_b1': _L1_xattn_in['b1'], 'L1_xattn_g2': _L1_xattn_in['g2'], 'L1_xattn_b2': _L1_xattn_in['b2'], 'L1_xattn_g3': _L1_xattn_in['g3'], 'L1_xattn_b3': _L1_xattn_in['b3']}

def reference(x, ctx_768, L0_xattn_ln1_g, L0_xattn_ln1_b, L0_xattn_ln2_g, L0_xattn_ln2_b, L0_xattn_ln3_g, L0_xattn_ln3_b, L0_xattn_sa_wq, L0_xattn_sa_bq, L0_xattn_sa_wk, L0_xattn_sa_bk, L0_xattn_sa_wv, L0_xattn_sa_bv, L0_xattn_sa_wo, L0_xattn_sa_bo, L0_xattn_ca_wq, L0_xattn_ca_bq, L0_xattn_ca_wk, L0_xattn_ca_bk, L0_xattn_ca_wv, L0_xattn_ca_bv, L0_xattn_ca_wo, L0_xattn_ca_bo, L0_xattn_mlp_w1, L0_xattn_mlp_b1, L0_xattn_mlp_w2, L0_xattn_mlp_b2, L1_xattn_Wq1, L1_xattn_Wk1, L1_xattn_Wv1, L1_xattn_Wo1, L1_xattn_bo1, L1_xattn_Wq2, L1_xattn_Wk2, L1_xattn_Wv2, L1_xattn_Wo2, L1_xattn_bo2, L1_xattn_Wp, L1_xattn_bp, L1_xattn_Wf, L1_xattn_bf, L1_xattn_g1, L1_xattn_b1, L1_xattn_g2, L1_xattn_b2, L1_xattn_g3, L1_xattn_b3):
    import jax
    import jax.numpy as jnp

    def _L0_xattn_ref(x, context, ln1_g, ln1_b, ln2_g, ln2_b, ln3_g, ln3_b, sa_wq, sa_bq, sa_wk, sa_bk, sa_wv, sa_bv, sa_wo, sa_bo, ca_wq, ca_bq, ca_wk, ca_bk, ca_wv, ca_bv, ca_wo, ca_bo, mlp_w1, mlp_b1, mlp_w2, mlp_b2):
        import jax, jax.numpy as jnp
        import numpy as np
        B, S, L = (2, 256, 64)
        WIDTH, HEADS, CTX = (128, 16, 96)
        HD = WIDTH // HEADS
        EPS = 1e-05

        def _layernorm(x, g, b):
            m = jnp.mean(x, axis=-1, keepdims=True)
            v = jnp.mean(jnp.square(x - m), axis=-1, keepdims=True)
            return (x - m) * jax.lax.rsqrt(v + EPS) * g + b

        def _mha(q_in, kv_in, wq, bq, wk, bk, wv, bv, wo, bo):
            b = q_in.shape[0]
            q = (q_in @ wq.T + bq).reshape(b, -1, HEADS, HD).transpose(0, 2, 1, 3)
            k = (kv_in @ wk.T + bk).reshape(b, -1, HEADS, HD).transpose(0, 2, 1, 3)
            v = (kv_in @ wv.T + bv).reshape(b, -1, HEADS, HD).transpose(0, 2, 1, 3)
            scores = jnp.einsum('bhqd,bhkd->bhqk', q, k) * HD ** (-0.5)
            p = jax.nn.softmax(scores, axis=-1)
            o = jnp.einsum('bhqk,bhkd->bhqd', p, v)
            o = o.transpose(0, 2, 1, 3).reshape(b, -1, WIDTH)
            return o @ wo.T + bo
        h = _layernorm(x, ln1_g, ln1_b)
        x = x + _mha(h, h, sa_wq, sa_bq, sa_wk, sa_bk, sa_wv, sa_bv, sa_wo, sa_bo)
        h = _layernorm(x, ln2_g, ln2_b)
        x = x + _mha(h, context, ca_wq, ca_bq, ca_wk, ca_bk, ca_wv, ca_bv, ca_wo, ca_bo)
        h = _layernorm(x, ln3_g, ln3_b)
        h = jax.nn.gelu(h @ mlp_w1.T + mlp_b1, approximate=False) @ mlp_w2.T + mlp_b2
        return x + h

    def _L1_xattn_ref(x, context, Wq1, Wk1, Wv1, Wo1, bo1, Wq2, Wk2, Wv2, Wo2, bo2, Wp, bp, Wf, bf, g1, b1, g2, b2, g3, b3):
        import jax, jax.numpy as jnp
        import numpy as np
        HEADS = 16
        D_HEAD = 64
        EPS = 1e-05

        def _ln(x, g, b):
            m = jnp.mean(x, axis=-1, keepdims=True)
            v = jnp.var(x, axis=-1, keepdims=True)
            return (x - m) * jax.lax.rsqrt(v + EPS) * g + b

        def _attn(xq, xc, Wq, Wk, Wv, Wo, bo):
            B, N, _ = xq.shape
            S = xc.shape[1]
            q = (xq @ Wq).reshape(B, N, HEADS, D_HEAD)
            k = (xc @ Wk).reshape(B, S, HEADS, D_HEAD)
            v = (xc @ Wv).reshape(B, S, HEADS, D_HEAD)
            scale = D_HEAD ** (-0.5)
            scores = jnp.einsum('bnhd,bshd->bhns', q, k) * scale
            attn = jax.nn.softmax(scores, axis=-1)
            out = jnp.einsum('bhns,bshd->bnhd', attn, v).reshape(B, N, HEADS * D_HEAD)
            return out @ Wo + bo

        def _geglu_ff(x, Wp, bp, Wf, bf):
            h = x @ Wp + bp
            a, gate = jnp.split(h, 2, axis=-1)
            return a * jax.nn.gelu(gate, approximate=False) @ Wf + bf
        x = _attn(_ln(x, g1, b1), _ln(x, g1, b1), Wq1, Wk1, Wv1, Wo1, bo1) + x
        x = _attn(_ln(x, g2, b2), context, Wq2, Wk2, Wv2, Wo2, bo2) + x
        x = _geglu_ff(_ln(x, g3, b3), Wp, bp, Wf, bf) + x
        return x
    x = _L0_xattn_ref(x, ctx_768, L0_xattn_ln1_g, L0_xattn_ln1_b, L0_xattn_ln2_g, L0_xattn_ln2_b, L0_xattn_ln3_g, L0_xattn_ln3_b, L0_xattn_sa_wq, L0_xattn_sa_bq, L0_xattn_sa_wk, L0_xattn_sa_bk, L0_xattn_sa_wv, L0_xattn_sa_bv, L0_xattn_sa_wo, L0_xattn_sa_bo, L0_xattn_ca_wq, L0_xattn_ca_bq, L0_xattn_ca_wk, L0_xattn_ca_bk, L0_xattn_ca_wv, L0_xattn_ca_bv, L0_xattn_ca_wo, L0_xattn_ca_bo, L0_xattn_mlp_w1, L0_xattn_mlp_b1, L0_xattn_mlp_w2, L0_xattn_mlp_b2)
    x = _L1_xattn_ref(x, ctx_768, L1_xattn_Wq1, L1_xattn_Wk1, L1_xattn_Wv1, L1_xattn_Wo1, L1_xattn_bo1, L1_xattn_Wq2, L1_xattn_Wk2, L1_xattn_Wv2, L1_xattn_Wo2, L1_xattn_bo2, L1_xattn_Wp, L1_xattn_bp, L1_xattn_Wf, L1_xattn_bf, L1_xattn_g1, L1_xattn_b1, L1_xattn_g2, L1_xattn_b2, L1_xattn_g3, L1_xattn_b3)
    return x

_drawn_inputs = setup_inputs


def setup_inputs(seed=0):
    import zlib

    import numpy as np

    out = dict(_drawn_inputs(seed))
    spreads = {'L0_xattn_ln1_g': (1.0, 0.6),
     'L0_xattn_ln1_b': (0.0, 0.1),
     'L0_xattn_ln2_g': (1.0, 0.6),
     'L0_xattn_ln2_b': (0.0, 0.8),
     'L0_xattn_ln3_g': (1.0, 0.6),
     'L0_xattn_ln3_b': (0.0, 0.8),
     'L0_xattn_sa_bq': (0.0, 0.8),
     'L0_xattn_sa_bk': (0.0, 2.0),
     'L0_xattn_sa_bv': (0.0, 0.1),
     'L0_xattn_sa_bo': (0.0, 0.1),
     'L0_xattn_ca_bq': (0.0, 0.736),
     'L0_xattn_ca_bk': (0.0, 2.0),
     'L0_xattn_ca_bv': (0.0, 0.1),
     'L0_xattn_ca_bo': (0.0, 0.1),
     'L0_xattn_mlp_b1': (0.0, 0.283),
     'L0_xattn_mlp_b2': (0.0, 0.1),
     'L1_xattn_bo1': (0.0, 0.1),
     'L1_xattn_bo2': (0.0, 0.1),
     'L1_xattn_bp': (0.0, 0.1),
     'L1_xattn_bf': (0.0, 0.1),
     'L1_xattn_g1': (1.0, 0.2),
     'L1_xattn_b1': (0.0, 0.1),
     'L1_xattn_g2': (1.0, 0.2),
     'L1_xattn_b2': (0.0, 0.343),
     'L1_xattn_g3': (1.0, 0.2),
     'L1_xattn_b3': (0.0, 0.1)}
    factors = {}
    for name, (base, spread) in spreads.items():
        noise = np.random.default_rng([zlib.crc32(name.encode()), seed]).standard_normal(out[name].shape)
        drawn = base * np.exp(spread * noise) if base else spread * noise
        out[name] = jnp.asarray(drawn.astype(out[name].dtype))
    for name, factor in factors.items():
        out[name] = (out[name] * factor).astype(out[name].dtype)
    return out
```

```python
from contextlib import ExitStack

import numpy as np

import concourse.bass as bass
import concourse.mybir as mybir

F32 = mybir.dt.float32
F32R = mybir.dt.float32r
BF16 = mybir.dt.bfloat16
ACT = mybir.ActivationFunctionType
ALU = mybir.AluOpType
AX_X = mybir.AxisListType.X

P = 128
BATCH, TOK, D = 4, 256, 128
KEYS, CTX = 64, 96
NE = 3
H = 16
HD0, HD1 = 8, 64
FF = 512
QT = TOK // P
PAIR = 2
LOOPS = BATCH // PAIR
HP = H // 2
NT0 = H // 4
EPS = 1e-5
SCALE0, SCALE1 = HD0 ** -0.5, HD1 ** -0.5
BANK = 512
HALF = 2 * BANK

W0_NAMES = ["wq0", "wk0", "wv0", "wo0", "cwq0", "cwo0", "w1", "w2"]
W0_COLS = dict(zip(W0_NAMES, [4 * P, 4 * P] + [P] * 4 + [FF, FF]))
W1_NAMES = ["wq1", "wk1", "wv1", "wo1", "wo2", "wp", "wf"]
W1_COLS = dict(zip(W1_NAMES, [1024] * 5 + [2 * FF, FF]))
VEC_NAMES = ["g0", "g1", "g2", "g3", "g4", "g5", "b0", "b1", "b2", "b3", "b4", "b5",
             "bqs", "bks", "cbq", "cbk", "bo0", "cbo0", "b1m", "b2m", "bo1", "bo2", "bp", "bf",
             "keep", "subq", "subk", "mask"]
VEC_COLS = dict(zip(VEC_NAMES, [1] * 12 + [4, 4] + [1] * 4 + [4, 1, 1, 1, 8, 1] + [1, 1, 1, H]))


def offsets(cols):
    out, at = {}, 0
    for name, n in cols.items():
        out[name] = at
        at += n
    return out, at


VEC_AT, VEC_N = offsets(VEC_COLS)
W0_AT, W0_N = offsets(W0_COLS)
W1_AT, W1_N = offsets(W1_COLS)


PHASES = ["sa0", "ca0", "ff0", "sa1", "ca1", "ff1"]


def steps(phase, j, *kinds):
    return [(k, phase, j, i) for k, n in kinds for i in range(n)]


def attend(score, value, phase, j, n_score, per_value):
    out, done = [], 0
    for c in range(n_score):
        out.append((score, phase, j, c))
        while (done + 1) * per_value <= c:
            out.append((value, phase, j, done))
            done += 1
    while done * per_value < n_score:
        out.append((value, phase, j, done))
        done += 1
    return out


def weave(main, fill):
    out, used = [], 0
    for n, s in enumerate(main):
        out.append(s)
        kind, i = s[0], s[3]
        if kind == "c0" and i % 2 == 0 or kind == "pv0" and i < 3 and main[n - 1][:1] == ("c0",) and main[n - 1][3] % 2 == 0:
            continue
        upto = len(fill) * (n + 1) // len(main)
        out += fill[used:upto]
        used = upto
    return out


def schedule():
    def self0_in(j):
        return steps("sa0", j, ("ln", 1), ("hT", 1), ("qk0", 1), ("v0", 1), ("b0", 8), ("m0", 1))

    def self0(j):
        return attend("c0", "pv0", "sa0", j, 8, 2)

    def self0_out(j):
        return steps("sa0", j, ("o0", 1), ("oT", 1), ("wo", 1), ("yT", 1))

    def cross0(j):
        return (steps("ca0", j, ("ck0", 1), ("ln", 1), ("hT", 1), ("q0c", 1), ("bc", 2), ("mc", 1), ("cc", 2),
                      ("pvc0", 2), ("o0", 1), ("oT", 1), ("wo", 1), ("yT", 1)))

    def ff0(j):
        return steps("ff0", j, ("ln", 1), ("hT", 1), ("w1", 1), ("wo", 1), ("yT", 1))

    def self1_in(j):
        out = steps("sa1", j, ("ln", 1), ("hT", 1))
        for i in range(HP):
            out += [("qk1", "sa1", j, i)]
            if i % 2:
                out += [("v1", "sa1", j, i // 2)]
            if i:
                out += [("b1", "sa1", j, i - 1)]
        return out + [("b1", "sa1", j, HP - 1), ("mc", "sa1", j, 0)]

    def self1(j):
        return attend("c1", "pv1", "sa1", j, HP, 1)

    def self1_out(j):
        return steps("sa1", j, ("o1", 4), ("wo", 1), ("yT", 1))

    def cross1(j):
        return (steps("ca1", j, ("ck1", 1), ("g1", 1), ("cv1", 1), ("ln", 1), ("hT", 1), ("bc", 2), ("mc", 1),
                      ("cc", 2), ("pvc1", HP), ("o1", 4), ("wo", 1), ("yT", 1)))

    def ff1(j):
        return steps("ff1", j, ("ln", 1), ("hT", 1), ("wp", 4), ("wo", 1), ("yT", 1))

    return (self0_in(0)
            + weave(self0(0), self0_in(1))
            + weave(self0(1), self0_out(0) + cross0(0) + ff0(0) + self1_in(0))
            + weave(self1(0), self0_out(1) + cross0(1) + ff0(1) + self1_in(1))
            + weave(self1(1), self1_out(0) + cross1(0) + ff1(0))
            + self1_out(1) + cross1(1) + ff1(1))


EXPS = ("c0", "c1", "cc")


def reader(step):
    kind, phase, j, c = step
    if kind == "c0":
        return "pv0", phase, j, c // 2
    if kind == "c1":
        return "pv1", phase, j, c
    return ("pvc0", phase, j, c) if phase == "ca0" else ("pvc1", phase, j, 4 * c + 3)


def slots_free(order):
    out, exps = [], []
    for s in order:
        if s in out:
            continue
        if s[0] in EXPS:
            if len(exps) >= NE and reader(exps[-NE]) not in out:
                kind, phase, j, i = reader(exps[-NE])
                out += [v for v in steps(phase, j, (kind, i + 1)) if v not in out]
                assert kind != "pv0" or exps[-1] == ("c0", phase, j, 2 * i + 1) or s != ("c0", phase, j, 2 * i + 1), s
            exps.append(s)
        out.append(s)
    return out


SCHEDULE = slots_free(schedule())
assert len(set(SCHEDULE)) == len(SCHEDULE)


def count_of(uses, step):
    n = uses.get(step[0], 0)
    return n(step) if callable(n) else n


class Tally:

    def __init__(self, credit=0, **incs):
        self.start, self.incs, n = {}, incs, 0
        for s in SCHEDULE:
            self.start[s] = n
            n += count_of(incs, s)
        self.total, self.credit = n, credit * n

    def at(self, loop, step, k=None, ago=0):
        k = count_of(self.incs, step) if k is None else k
        return loop * self.total + (self.credit - ago * self.total + self.start[step] + k)


class Ring:

    def __init__(self, size, **uses):
        self.size, self.first, n = size, {}, 0
        for s in SCHEDULE:
            self.first[s] = n
            n += count_of(uses, s)
        assert n % size == 0, (n, uses)
        self.per_slot = n // size

    def slot(self, step, k=0):
        return (self.first[step] + k) % self.size

    def nth(self, loop, step, k=0):
        return loop * self.per_slot + ((self.first[step] + k) // self.size + 1)

    def full_credited(self, loop, step, ago=0):
        return loop * self.per_slot + ((1 - ago) * self.per_slot + self.first[step] // self.size + 1)

    def taken(self, loop, step, k=0):
        return loop * self.per_slot + ((self.first[step] + k) // self.size + 2)


def build(nc, x_in, ctx_in, w0_in, w1_in, kv0_in, kv1_in, vec_in, bv_in, id_in, sel_in, out):
    ln_n = Tally(ln=7)
    rstd_n = Tally(ln=1)
    h_n = Tally(hT=2)
    hi_n = Tally(oT=1, o1=1, q0c=1, qk1=1, g1=2, wp=1)
    stack_n = Tally(qk0=8)
    pool_n = Tally(v0=2, qk0=1, hT=lambda s: s[1] in ("ca0", "sa1", "ca1"), v1=lambda s: s[3] == 0,
                   ck0=3, ck1=1, cv1=3)
    max_n = Tally(b0=1, b1=1, bc=1, mc=2)
    norm_n = Tally(o0=2, pv1=1, pvc1=1)
    g_n = Tally(w1=4, wp=2)
    kc_n = Tally(ck0=6, ck1=1, cv1=2)
    pv_n = Tally(credit=1, pv0=lambda s: s[3] % 2 == 0)
    turns = Ring(2, hT=1, qk0=4, v0=1, m0=2, o0=2, oT=1, wo=1, yT=1, ck0=1, q0c=1, mc=1, w1=2,
                 qk1=1, v1=1, o1=1, ck1=1, g1=2, cv1=2, wp=1)
    scores = Ring(2, b0=1, c0=1, b1=1, c1=1, bc=1, cc=1)
    outs = Ring(2, pv1=1, pvc1=1, pvc0=1, pv0=lambda s: s[3] % 2)

    exps = [s for s in SCHEDULE if s[0] in EXPS]
    slot_of = {s: n % NE for n, s in enumerate(exps)}
    last_reader, seen = {}, {}
    for s in exps:
        if slot_of[s] in seen:
            last_reader[s] = (reader(seen[slot_of[s]]), 0)
        seen[slot_of[s]] = s
    for s in exps[:NE]:
        last_reader[s] = (reader(seen[slot_of[s]]), 1)

    ctx = ExitStack()
    with ctx:
        def sb(name, shape, dt=F32):
            return ctx.enter_context(nc.sbuf_tensor(name, shape, dt))

        def sem(name):
            return ctx.enter_context(nc.semaphore(name))

        w0h, w0l = sb("w0h", [P, W0_N], F32R), sb("w0l", [P, W0_N], F32R)
        w1h, w1l = sb("w1h", [P, W1_N], F32R), sb("w1l", [P, W1_N], F32R)
        kv0 = sb("kv0", [CTX, 2 * D])
        kv1 = sb("kv1", [P, 3, 1024])
        vec = sb("vec", [P, VEC_N])
        bv = sb("bv", [P, 2, D])
        ident = sb("ident", [P, P])
        select = sb("select", [P, HP * P], BF16)
        identb = sb("identb", [P, P], BF16)
        halfneg = sb("halfneg", [P, QT])
        x = [sb(f"x{j}", [P, QT, D]) for j in range(PAIR)]
        yT = [sb(f"yT{j}", [P, TOK]) for j in range(PAIR)]
        hh = [sb(f"hh{j}", [P, TOK], F32R) for j in range(PAIR)]
        hl = [sb(f"hl{j}", [P, TOK], F32R) for j in range(PAIR)]
        aug = [sb(f"aug{j}", [P, TOK], BF16) for j in range(PAIR)]
        qkh = [sb(f"qkh{j}", [P, 4096], F32R) for j in range(PAIR)]
        qkl = [sb(f"qkl{j}", [P, 4096], F32R) for j in range(PAIR)]
        vv = [sb(f"vv{j}", [P, QT * H * (HD1 + 1)]) for j in range(PAIR)]
        on = [sb(f"on{j}", [P, QT * H * HD1]) for j in range(PAIR)]
        ct = [sb(f"ct{j}", [CTX, 2, KEYS]) for j in range(PAIR)]
        stats = [sb(f"stats{j}", [P, QT, 6]) for j in range(PAIR)]
        mv = [sb(f"mv{j}", [P, QT, 2]) for j in range(PAIR)]
        ve = [sb(f"ve{j}", [P, QT]) for j in range(PAIR)]
        rstd = [sb(f"rstd{j}", [P, QT]) for j in range(PAIR)]
        rden = [sb(f"rden{j}", [P, QT * H]) for j in range(PAIR)]
        probs = sb("probs", [P, NE, HALF])

        tp = [ctx.enter_context(nc.psum_tensor(f"tp{i}", [P, BANK], F32)) for i in range(2)]
        sc = [ctx.enter_context(nc.psum_tensor(f"sc{i}", [P, 2, BANK], F32)) for i in range(2)]
        ov = [ctx.enter_context(nc.psum_tensor(f"ov{i}", [P, BANK], F32)) for i in range(2)]

        x_loaded = [sem(f"x_loaded{j}") for j in range(PAIR)]
        w0_loaded, w1_loaded, wn_loaded, small_loaded = sem("w0_loaded"), sem("w1_loaded"), sem("wn_loaded"), sem("small_loaded")
        w0_hi, w0_lo, w1_hi, w1_lo = sem("w0_hi"), sem("w0_lo"), sem("w1_hi"), sem("w1_lo")
        consts_set = sem("consts_set")
        pool_passed, dve_passed = sem("pool_passed"), sem("dve_passed")
        stored = sem("stored")
        tp_full = [sem(f"tp_full{i}") for i in range(2)]
        tp_taken = [sem(f"tp_taken{i}") for i in range(2)]
        sc_full = [sem(f"sc_full{i}") for i in range(2)]
        sc_taken = [sem(f"sc_taken{i}") for i in range(2)]
        ov_full = [sem(f"ov_full{i}") for i in range(2)]
        ov_taken = [sem(f"ov_taken{i}") for i in range(2)]
        pv_done = sem("pv_done")
        ln_step = sem("ln_step")
        rstd_set = sem("rstd_set")
        h_split = sem("h_split")
        hi_set = sem("hi_set")
        stack_step = sem("stack_step")
        pool_set = sem("pool_set")
        max_set = sem("max_set")
        norm_step = sem("norm_step")
        g_step = sem("g_step")
        kc_step = sem("kc_step")

        def v(name, i=0, n=1):
            at = VEC_AT[name] + i
            return vec[:, at:at + n]

        def w(hi_lo, name, a, b):
            tile, at = ((w0h, w0l), W0_AT) if name in W0_AT else ((w1h, w1l), W1_AT)
            return tile[hi_lo][:, at[name] + a:at[name] + b]

        def qs(j):
            return qkh[j][:, 0:1024].rearrange("p (t q) -> p t q", t=NT0)

        def qm(j):
            return qkh[j][:, 1024:2048].rearrange("p (t q) -> p t q", t=NT0)

        def ks(j):
            return qkh[j][:, 2048:3072].rearrange("p (t q) -> p t q", t=NT0)

        def qk(tile, j, jj, which):
            a = (jj * 2 + which) * TOK
            return tile[j][:, a:a + TOK]

        def g_of(tile, j):
            return tile[j][:, 2048:3072]

        def v32(j):
            return vv[j][:, 0:1024].rearrange("p (t h c) -> p t h c", t=QT, h=H)

        def v65(j):
            return vv[j][:, :].rearrange("p (t h c) -> p t h c", t=QT, h=H)

        def vb0(j):
            return vv[j][:, 0:512].rearrange("p (w c) -> p w c", w=HP)

        def vb1(j):
            return vv[j][:, 0:HP * 130].rearrange("p (w c) -> p w c", w=HP)

        def mx0(j):
            return on[j][:, 0:1024].rearrange("p (t n c) -> p t n c", t=QT, n=NT0)

        def mxc(j):
            return on[j][:, 0:P].bitcast(BF16).rearrange("p (t c) -> p t c", t=QT)

        def raw_max(j):
            return rden[j][:].rearrange("p (t g w) -> p t g w", t=QT, g=2)

        def oT0(j):
            return on[j][:, 1024:2048]

        def crossq(j, phase):
            return (qkh[j][:, 0:TOK], qkl[j][:, 0:TOK]) if phase == "ca0" else (hh[j], hl[j])

        def spread(ap, n):
            return ap.unsqueeze(len(ap.shape)).broadcast_to([*ap.shape, n])

        raw0 = probs[:].rearrange("p e n -> p (e n)")[:, 0:W0_N]
        raw1 = [on[1][:], vv[1][:, 0:2048], on[0][:], vv[0][:, 1024:1536]]
        raw1_at = [0, 2048, 4096, 6144]

        block = ctx.enter_context(nc.Block())

        @block.sync
        def _(sp):
            sp.dma_start(vec[:], vec_in).then_inc(small_loaded, 16)
            sp.dma_start(ident[:], id_in).then_inc(small_loaded, 16)
            sp.dma_start(bv[:].rearrange("p a d -> p (a d)"), bv_in.partition_broadcast(P)).then_inc(small_loaded, 16)
            sp.dma_start(vv[0][:, 0:HP * P], sel_in).then_inc(small_loaded, 16)
            sp.sem_inc(stored, 16)
            with sp.Fori(0, LOOPS) as loop:
                sp.wait_ge(stored, loop * (16 * PAIR) + 16)
                for j in range(PAIR):
                    sp.dma_start(x[j][:], x_in[loop * PAIR + j].rearrange("(t p) d -> p t d", p=P)).then_inc(x_loaded[j], 16)
                    for twice in range(2):
                        sp.dma_start(ct[j][:, twice, :], ctx_in[loop * PAIR + j]).then_inc(x_loaded[j], 16)
                for j in range(PAIR):
                    last = ("yT", "ff1", j, 0)
                    sp.wait_ge(tp_taken[turns.slot(last)], turns.taken(loop, last))
                    sp.dma_start(out[loop * PAIR + j].rearrange("(t p) d -> p t d", p=P), x[j][:]).then_inc(stored, 16)
            sp.wait_ge(stored, 16 * BATCH + 16)

        @block.scalar
        def _(act):
            act.dma_start(raw0, w0_in).then_inc(w0_loaded, 16)
            act.dma_start(kv0[:], kv0_in).then_inc(wn_loaded, 16)
            for raw, at in zip(raw1, raw1_at):
                act.dma_start(raw, w1_in[:, at:at + raw.shape[1]]).then_inc(w1_loaded, 16)
            act.dma_start(kv1[:].rearrange("p a n -> p (a n)"), kv1_in).then_inc(wn_loaded, 16)
            act.wait_ge(w0_loaded, 16)
            act.activation(w0h[:], raw0, ACT.Copy).then_inc(w0_hi, 1)
            act.wait_ge(small_loaded, 64)
            act.activation(select[:], vv[0][:, 0:HP * P], ACT.Copy).then_inc(w0_hi, 1)
            act.wait_ge(w1_loaded, 64)
            for raw, at in zip(raw1, raw1_at):
                act.activation(w1h[:, at:at + raw.shape[1]], raw, ACT.Copy).then_inc(w1_hi, 1)
            act.wait_ge(w0_lo, 1)
            act.wait_ge(w1_lo, 4)
            with act.Fori(0, LOOPS) as loop:
                def full_tile(step, k=0):
                    s = turns.slot(step, k)
                    act.wait_ge(tp_full[s], turns.nth(loop, step, k))
                    return tp[s], tp_taken[s]

                for step in SCHEDULE:
                    kind, phase, j, i = step
                    if kind == "hT":
                        n = PHASES.index(phase)
                        ps, taken = full_tile(step)
                        act.activation(yT[j][:], ps[:, 0:TOK], ACT.Identity, bias=v(f"b{n}"), scale=v(f"g{n}")).then_inc(taken, 1)
                    elif kind == "qk0":
                        for k in range(4):
                            ps, taken = full_tile(step, k)
                            for t in range(2):
                                ins = act.activation(on[j][:, k * BANK + t * TOK:k * BANK + (t + 1) * TOK], ps[:, t * TOK:(t + 1) * TOK], ACT.Identity,
                                                     bias=v("bqs" if k < 2 else "bks", 2 * (k % 2) + t), scale=v("keep"))
                            ins.then_inc(taken, 1)
                    elif kind in ("c0", "c1", "cc"):
                        s = scores.slot(step)
                        reading, ago = last_reader[step]
                        if count_of(pv_n.incs, reading):
                            act.wait_ge(pv_done, pv_n.at(loop, reading, ago=ago))
                        else:
                            act.wait_ge(ov_full[outs.slot(reading)], outs.full_credited(loop, reading, ago))
                        act.wait_ge(sc_full[s], scores.nth(loop, step))
                        act.activation(probs[:, slot_of[step], :], sc[s][:].rearrange("p b n -> p (b n)"), ACT.Exp,
                                       scale=SCALE0 if phase in ("sa0", "ca0") else SCALE1).then_inc(sc_taken[s], 1)
                    elif (kind == "pv0" and i % 2) or kind == "pvc0":
                        s, half = outs.slot(step), i // 2 if kind == "pv0" else i
                        act.wait_ge(ov_full[s], outs.full_credited(loop, step))
                        act.activation(oT0(j)[:, half * BANK:(half + 1) * BANK], ov[s][:], ACT.Copy).then_inc(ov_taken[s], 1)
                    elif kind == "mc":
                        ps, taken = full_tile(step)
                        act.activation(aug[j][:], ps[:, 0:P].bitcast(BF16), ACT.Copy).then_inc(taken, 1)
                    elif kind in ("oT", "q0c"):
                        ps, _ = full_tile(step)
                        bias = v("cbq") if kind == "q0c" else 0.0
                        act.activation(qkh[j][:, 0:TOK], ps[:, 0:TOK], ACT.Identity, bias=bias).then_inc(hi_set, 1)
                    elif kind in ("qk1", "o1"):
                        ps, _ = full_tile(step)
                        act.activation(qkh[j][:, i * BANK:(i + 1) * BANK], ps[:], ACT.Copy).then_inc(hi_set, 1)
                    elif kind == "g1":
                        for k in range(2):
                            ps, _ = full_tile(step, k)
                            act.activation(g_of(qkh, j)[:, k * BANK:(k + 1) * BANK], ps[:], ACT.Copy).then_inc(hi_set, 1)
                    elif kind == "w1":
                        for k in range(2):
                            ps, taken = full_tile(step, k)
                            for t in range(2):
                                ins = act.activation(on[j][:, k * BANK + t * TOK:k * BANK + (t + 1) * TOK], ps[:, t * TOK:(t + 1) * TOK], ACT.Gelu,
                                                     bias=v("b1m", 2 * k + t))
                            ins.then_inc(taken, 1)
                    elif kind == "wp":
                        ps, _ = full_tile(step)
                        act.activation(on[j][:, 1024 + i * TOK:1024 + (i + 1) * TOK], ps[:, TOK:2 * TOK], ACT.Gelu, bias=v("bp", 4 + i)).then_inc(hi_set, 1)
                    elif kind == "wo":
                        ps, taken = full_tile(step)
                        bias = {"sa0": "bo0", "ca0": "cbo0", "ff0": "b2m", "sa1": "bo1", "ca1": "bo2", "ff1": "bf"}[phase]
                        act.activation(yT[j][:], ps[:, 0:TOK], ACT.Identity, bias=v(bias)).then_inc(taken, 1)

        @block.gpsimd
        def _(pool):
            pool.memset(halfneg[:], -0.5).then_inc(consts_set, 1)
            pool.wait_ge(consts_set, 1)
            pool.wait_ge(w1_hi, 4)
            pool.wait_ge(w1_lo, 4)
            pool.wait_ge(w0_hi, 2)
            with pool.Fori(0, LOOPS) as loop:
                for step in SCHEDULE:
                    kind, phase, j, i = step

                    def settled():
                        pool.sem_inc(pool_passed, 1)

                    def behind(k=0):
                        s = turns.slot(step, k)
                        pool.wait_ge(tp_full[s], turns.nth(loop, step, k))
                        settled()

                    if kind == "ln":
                        pool.wait_ge(ln_step, ln_n.at(loop, step, 5))
                        pool.tensor_tensor(rstd[j][:], ve[j][:], halfneg[:], ALU.pow).then_inc(rstd_set, 1)
                    elif kind == "hT" and count_of(pool_n.incs, step):
                        behind()
                        pool.memset(on[j][:, 0:P], 0.0).then_inc(pool_set, 1)
                    elif kind == "qk0":
                        pool.wait_ge(stack_step, stack_n.at(loop, step))
                        settled()
                        pool.memset(on[j][:, 0:1024], 0.0).then_inc(pool_set, 1)
                    elif kind == "v0":
                        behind()
                        pool.memset(vv[j][:, 0:1024], 0.0).then_inc(pool_set, 1)
                        pool.wait_ge(pool_set, pool_n.at(loop, step, 1))
                        settled()
                        pool.memset(v32(j)[:, :, :, HD0:HD0 + 1], 1.0).then_inc(pool_set, 1)
                    elif kind == "v1" and i == 0:
                        behind()
                        pool.memset(v65(j)[:, :, :, HD1:HD1 + 1], 1.0).then_inc(pool_set, 1)
                    elif kind == "ck0":
                        behind()
                        pool.memset(vv[j][:, 0:512], 0.0).then_inc(pool_set, 1)
                        pool.wait_ge(pool_set, pool_n.at(loop, step, 1))
                        settled()
                        pool.memset(vb0(j)[0:KEYS, :, 8:9], 1.0).then_inc(pool_set, 1)
                        pool.memset(vb0(j)[KEYS:P, :, 40:41], 1.0).then_inc(pool_set, 1)
                    elif kind == "ck1":
                        behind()
                        pool.memset(on[j][:, 0:1024], 0.0).then_inc(pool_set, 1)
                    elif kind == "cv1":
                        behind()
                        pool.memset(vv[j][:, 0:HP * 130], 0.0).then_inc(pool_set, 1)
                        pool.wait_ge(pool_set, pool_n.at(loop, step, 1))
                        settled()
                        pool.memset(vb1(j)[0:KEYS, :, 64:65], 1.0).then_inc(pool_set, 1)
                        pool.memset(vb1(j)[KEYS:P, :, 129:130], 1.0).then_inc(pool_set, 1)

        @block.vector
        def _(dve):
            dve.wait_ge(w0_loaded, 16)
            dve.wait_ge(w0_hi, 1)
            dve.tensor_tensor(w0l[:], raw0, w0h[:].bitcast(F32), ALU.subtract).then_inc(w0_lo, 1)
            for k, (raw, at) in enumerate(zip(raw1, raw1_at)):
                dve.wait_ge(w1_hi, k + 1)
                cols = slice(at, at + raw.shape[1])
                dve.tensor_tensor(w1l[:, cols], raw, w1h[:, cols].bitcast(F32), ALU.subtract).then_inc(w1_lo, 1)
            dve.wait_ge(small_loaded, 64)
            dve.tensor_copy(identb[:], ident[:]).then_inc(w0_lo, 1)
            for s in (*tp_taken, *sc_taken, *ov_taken):
                dve.sem_inc(s, 1)
            for s in ov_full:
                dve.sem_inc(s, outs.per_slot)
            dve.sem_inc(pv_done, pv_n.total)
            with dve.Fori(0, LOOPS) as loop:
                def full_tile(step, k=0):
                    s = turns.slot(step, k)
                    dve.wait_ge(tp_full[s], turns.nth(loop, step, k))
                    return tp[s], tp_taken[s]

                def taken_tile(step, k=0):
                    s = turns.slot(step, k)
                    dve.wait_ge(tp_taken[s], turns.taken(loop, step, k))

                def low_part(step, cols, n, k=0, bias=None, at=0):
                    j = step[2]
                    ps, taken = full_tile(step, k)
                    dve.wait_ge(hi_set, hi_n.at(loop, step, k + 1))
                    hi = qkh[j][:, at:at + n].bitcast(F32)
                    if bias is None:
                        dve.tensor_tensor(qkl[j][:, at:at + n], ps[:, 0:n], hi, ALU.subtract).then_inc(taken, 1)
                    else:
                        dve.scalar_tensor_tensor(qkl[j][:, at:at + n], ps[:, 0:n], bias, hi, ALU.add, ALU.subtract).then_inc(taken, 1)

                for step in SCHEDULE:
                    kind, phase, j, i = step
                    if kind == "ln":
                        if phase == "sa0":
                            dve.wait_ge(x_loaded[j], loop * 48 + 48)
                        else:
                            taken_tile(("yT", PHASES[PHASES.index(phase) - 1], j, 0))
                        for t in range(QT):
                            dve.bn_stats(stats[j][:, t, :], x[j][:, t, :]).then_inc(ln_step, 1)
                        dve.wait_ge(ln_step, ln_n.at(loop, step, 2))
                        dve.sem_inc(dve_passed, 1)
                        for t in range(QT):
                            dve.bn_aggr(mv[j][:, t, :], stats[j][:, t, :]).then_inc(ln_step, 1)
                        dve.wait_ge(ln_step, ln_n.at(loop, step, 4))
                        dve.tensor_scalar(ve[j][:], mv[j][:, :, 1], EPS, None, ALU.add).then_inc(ln_step, 1)
                        dve.wait_ge(rstd_set, rstd_n.at(loop, step))
                        for t in range(QT):
                            dve.tensor_scalar(yT[j][:, t * P:(t + 1) * P], x[j][:, t, :], mv[j][:, t, 0:1], rstd[j][:, t:t + 1],
                                              ALU.subtract, ALU.mult).then_inc(ln_step, 1)
                    elif kind == "hT":
                        taken_tile(step)
                        dve.tensor_copy(hh[j][:], yT[j][:]).then_inc(h_split, 1)
                        dve.wait_ge(h_split, h_n.at(loop, step, 1))
                        dve.tensor_tensor(hl[j][:], yT[j][:], hh[j][:].bitcast(F32), ALU.subtract).then_inc(h_split, 1)
                    elif kind == "qk0":
                        for k in range(4):
                            taken_tile(step, k)
                            val = on[j][:, k * BANK:(k + 1) * BANK]
                            hi = qkl[j][:, k * BANK:(k + 1) * BANK]
                            dst = (qs if k < 2 else ks)(j)[:, 2 * (k % 2):2 * (k % 2) + 2, :].rearrange("p t q -> p (t q)")
                            dve.tensor_copy(hi, val).then_inc(stack_step, 1)
                            dve.wait_ge(stack_step, stack_n.at(loop, step, 2 * k + 1))
                            dve.scalar_tensor_tensor(dst, hi.bitcast(F32), v("subq" if k < 2 else "subk"), val,
                                                     ALU.mult, ALU.add).then_inc(stack_step, 1)
                    elif kind == "v0":
                        dve.wait_ge(pool_set, pool_n.at(loop, step))
                        ps, taken = full_tile(step)
                        dve.tensor_tensor(v32(j)[:, :, :, 0:HD0], ps[:, 0:TOK].rearrange("p (t h d) -> p t h d", t=QT, h=H),
                                          bv[:, 0, :].rearrange("p (h d) -> p h d", h=H).unsqueeze(1).broadcast_to([P, QT, H, HD0]),
                                          ALU.add).then_inc(taken, 1)
                    elif kind in ("b0", "b1"):
                        s = scores.slot(step)
                        dve.wait_ge(sc_full[s], scores.nth(loop, step))
                        if kind == "b0":
                            dve.wait_ge(pool_set, pool_n.at(loop, ("qk0", phase, j, 0)))
                            t, g = i // 2, 2 * (i % 2)
                            dst = mx0(j)[:, :, t, :].rearrange("p q (g c) -> p g q c", g=4)[:, g:g + 2, :, 24]
                        else:
                            dst = raw_max(j)[:, :, :, i].rearrange("p q g -> p g q")
                        dve.tensor_reduce(dst, sc[s][:].rearrange("p g (q k) -> p g q k", q=QT), AX_X, ALU.max,
                                          negate=True).then_inc(max_set, 1)
                        dve.wait_ge(max_set, max_n.at(loop, step))
                        dve.sem_inc(sc_taken[s], 1)
                    elif kind == "bc":
                        s = scores.slot(step)
                        dve.wait_ge(sc_full[s], scores.nth(loop, step))
                        dst = raw_max(j)[:, i].rearrange("p g w -> p w g")
                        dve.tensor_reduce(dst, sc[s][:].rearrange("p b (w g k) -> p (b w) g k", g=2, k=KEYS), AX_X, ALU.max,
                                          negate=True).then_inc(max_set, 1)
                        dve.wait_ge(max_set, max_n.at(loop, step))
                        dve.sem_inc(sc_taken[s], 1)
                    elif kind == "mc":
                        dve.wait_ge(pool_set, pool_n.at(loop, ("hT", phase, j, 0)))
                        hi, lo = (mxc(j).rearrange("p q (g c) -> p q g c", g=2)[:, :, :, a:a + HP] for a in (0, HP))
                        dve.tensor_copy(hi, raw_max(j)).then_inc(max_set, 1)
                        dve.wait_ge(max_set, max_n.at(loop, step, 1))
                        dve.tensor_tensor(lo, raw_max(j), hi, ALU.subtract).then_inc(max_set, 1)
                    elif kind == "m0":
                        for k in range(2):
                            ps, taken = full_tile(step, k)
                            cols = slice(k * BANK, (k + 1) * BANK)
                            dve.tensor_tensor(qm(j).rearrange("p t q -> p (t q)")[:, cols], qs(j).rearrange("p t q -> p (t q)")[:, cols].bitcast(F32),
                                              ps[:], ALU.add).then_inc(taken, 1)
                    elif kind == "o0":
                        for k in range(QT):
                            ps, taken = full_tile(step, k)
                            o = ps[:].rearrange("p (h c) -> p h c", h=H)
                            den = rden[j][:, k * H:(k + 1) * H]
                            dve.reciprocal(den, o[:, :, HD0]).then_inc(norm_step, 1)
                            dve.wait_ge(norm_step, norm_n.at(loop, step, k + 1))
                            dve.tensor_tensor(on[j][:, k * P:(k + 1) * P].rearrange("p (h d) -> p h d", h=H), o[:, :, 0:HD0],
                                              spread(den, HD0), ALU.mult).then_inc(taken, 1)
                    elif kind in ("pv1", "pvc1"):
                        s = outs.slot(step)
                        dve.wait_ge(ov_full[s], outs.full_credited(loop, step))
                        order = "p (g t c) -> p g t c" if kind == "pv1" else "p (t g c) -> p g t c"
                        o = ov[s][:, 0:4 * 65].rearrange(order, g=2, t=QT)
                        den = rden[j][:, 4 * i:4 * i + 4].rearrange("p (g t) -> p g t", g=2)
                        dve.reciprocal(den, o[:, :, :, HD1]).then_inc(norm_step, 1)
                        dve.wait_ge(norm_step, norm_n.at(loop, step))
                        dst = on[j][:].rearrange("p (t h d) -> p h t d", t=QT, h=H)[:, 2 * i:2 * i + 2]
                        dve.tensor_tensor(dst, o[:, :, :, 0:HD1], spread(den, HD1), ALU.mult).then_inc(ov_taken[s], 1)
                    elif kind == "oT":
                        low_part(step, None, TOK)
                    elif kind == "q0c":
                        low_part(step, None, TOK, bias=v("cbq"))
                    elif kind in ("qk1", "o1"):
                        low_part(step, None, BANK, at=i * BANK)
                    elif kind == "g1":
                        for k in range(2):
                            low_part(step, None, BANK, k=k, at=2048 + k * BANK)
                    elif kind == "v1":
                        ps, taken = full_tile(step)
                        t, half = divmod(i, 2)
                        dve.tensor_copy(v65(j)[:, t, half * 8:half * 8 + 8, 0:HD1], ps[:].rearrange("p (h d) -> p h d", h=8)).then_inc(taken, 1)
                    elif kind == "yT":
                        ps, taken = full_tile(step)
                        dve.tensor_tensor(x[j][:].rearrange("p t d -> p (t d)"), x[j][:].rearrange("p t d -> p (t d)"), ps[:, 0:TOK],
                                          ALU.add).then_inc(taken, 1)
                    elif kind == "ck0":
                        ps, taken = full_tile(step)
                        dve.tensor_scalar(yT[j][:, 0:KEYS], ps[:, 0:KEYS], v("cbk"), None, ALU.add).then_inc(kc_step, 1)
                        dve.wait_ge(kc_step, kc_n.at(loop, step, 1))
                        dve.tensor_copy(hh[j][:, 0:KEYS], yT[j][:, 0:KEYS]).then_inc(kc_step, 1)
                        dve.wait_ge(kc_step, kc_n.at(loop, step, 2))
                        dve.tensor_tensor(hl[j][:, 0:KEYS], yT[j][:, 0:KEYS], hh[j][:, 0:KEYS].bitcast(F32), ALU.subtract).then_inc(kc_step, 1)
                        dve.wait_ge(pool_set, pool_n.at(loop, step))
                        val = ps[:, KEYS:KEYS + D].rearrange("p (w g d) -> p w g d", g=2, d=HD0)
                        bias = bv[:, 1, :].rearrange("p (w g d) -> p w g d", g=2, d=HD0)
                        dve.tensor_tensor(vb0(j)[0:KEYS, :, 0:HD0], val[0:KEYS, :, 0, :], bias[0:KEYS, :, 0, :], ALU.add).then_inc(kc_step, 1)
                        dve.tensor_tensor(vb0(j)[KEYS:P, :, 32:32 + HD0], val[KEYS:P, :, 1, :], bias[KEYS:P, :, 1, :], ALU.add).then_inc(taken, 1)
                        dve.wait_ge(kc_step, kc_n.at(loop, step, 4))
                        mask = spread(v("mask", 0, H), KEYS)
                        for part, dst in ((hh[j][:, 0:KEYS].bitcast(F32), g_of(qkh, j)), (hl[j][:, 0:KEYS].bitcast(F32), g_of(qkl, j))):
                            dve.tensor_tensor(dst.rearrange("p (h k) -> p h k", h=H), part.unsqueeze(1).broadcast_to([P, H, KEYS]), mask,
                                              ALU.mult).then_inc(kc_step, 1)
                    elif kind == "ck1":
                        ps, taken = full_tile(step)
                        dve.wait_ge(pool_set, pool_n.at(loop, step))
                        dst = on[j][:, 0:1024].rearrange("p (w c) -> p w c", w=HP)
                        src = ps[:].rearrange("p (w k) -> p w k", w=HP)
                        dve.tensor_copy(dst[0:KEYS, :, 0:KEYS], src[0:KEYS]).then_inc(kc_step, 1)
                        dve.tensor_copy(dst[KEYS:P, :, KEYS:P], src[KEYS:P]).then_inc(taken, 1)
                    elif kind == "cv1":
                        for k in range(2):
                            ps, taken = full_tile(step, k)
                            if k == 0:
                                dve.wait_ge(pool_set, pool_n.at(loop, step))
                            src = ps[:].rearrange("p (w g d) -> p w g d", g=2, d=HD1)
                            dst = vb1(j)[:, 4 * k:4 * k + 4, :]
                            dve.tensor_copy(dst[0:KEYS, :, 0:HD1], src[0:KEYS, :, 0, :]).then_inc(kc_step, 1)
                            dve.tensor_copy(dst[KEYS:P, :, 65:65 + HD1], src[KEYS:P, :, 1, :]).then_inc(taken, 1)
                    elif kind == "w1":
                        for k in range(2):
                            taken_tile(step, k)
                            cols = slice(k * BANK, (k + 1) * BANK)
                            dve.tensor_copy(qkh[j][:, cols], on[j][:, cols]).then_inc(g_step, 1)
                            dve.wait_ge(g_step, g_n.at(loop, step, 2 * k + 1))
                            dve.tensor_tensor(qkl[j][:, cols], on[j][:, cols], qkh[j][:, cols].bitcast(F32), ALU.subtract).then_inc(g_step, 1)
                    elif kind == "wp":
                        ps, taken = full_tile(step)
                        dve.wait_ge(hi_set, hi_n.at(loop, step))
                        cols = slice(i * TOK, (i + 1) * TOK)
                        dve.scalar_tensor_tensor(on[j][:, cols], ps[:, 0:TOK], v("bp", i), on[j][:, 1024 + i * TOK:1024 + (i + 1) * TOK],
                                                 ALU.add, ALU.mult).then_inc(taken, 1)
                        taken_tile(step)
                        dve.tensor_copy(qkh[j][:, cols], on[j][:, cols]).then_inc(g_step, 1)
                        dve.wait_ge(g_step, g_n.at(loop, step, 1))
                        dve.tensor_tensor(qkl[j][:, cols], on[j][:, cols], qkh[j][:, cols].bitcast(F32), ALU.subtract).then_inc(g_step, 1)

        @block.tensor
        def _(pe):
            pe.wait_ge(w0_hi, 2)
            pe.wait_ge(w0_lo, 2)
            pe.wait_ge(small_loaded, 64)
            pe.wait_ge(wn_loaded, 32)
            pe.wait_ge(w1_hi, 4)
            pe.wait_ge(w1_lo, 4)

            def three(dst, a, b, start=True, stop=True):
                passes = ((0, 0), (0, 1), (1, 0))
                for n, (p, q) in enumerate(passes):
                    ins = pe.matmul(dst, a[p], b[q], start=start and n == 0, stop=stop and n == 2)
                return ins

            with pe.Fori(0, LOOPS) as loop:
                def taken_tiles(*uses, but=None):
                    for s, use in {turns.slot(*use): use for use in uses}.items():
                        if s != but:
                            pe.wait_ge(tp_taken[s], turns.taken(loop, *use))

                def free_tile(step, k=0, after=()):
                    s = turns.slot(step, k)
                    taken_tiles(*after, but=s)
                    pe.wait_ge(tp_taken[s], turns.nth(loop, step, k))
                    return tp[s], tp_full[s]

                for step in SCHEDULE:
                    kind, phase, j, i = step
                    hid = (hh[j], hl[j])
                    if kind == "hT":
                        pe.wait_ge(ln_step, ln_n.at(loop, ("ln", phase, j, 0)))
                        ps, full = free_tile(step)
                        for t in range(QT):
                            ins = pe.transpose(ps[:, t * P:(t + 1) * P], yT[j][:, t * P:(t + 1) * P], ident[:])
                        ins.then_inc(full, 1)
                    elif kind == "qk0":
                        pe.wait_ge(h_split, h_n.at(loop, ("hT", phase, j, 0)))
                        for k in range(4):
                            ps, full = free_tile(step, k)
                            for t in range(2):
                                a = P * (2 * (k % 2) + t)
                                wide = [w(n, "wq0" if k < 2 else "wk0", a, a + P) for n in range(2)]
                                ins = three(ps[:, t * TOK:(t + 1) * TOK], wide, (hh[j][:], hl[j][:]))
                            ins.then_inc(full, 1)
                    elif kind == "v0":
                        ps, full = free_tile(step)
                        for t in range(QT):
                            a = slice(t * P, (t + 1) * P)
                            ins = three(ps[:, a], (hh[j][:, a], hl[j][:, a]), (w(0, "wv0", 0, D), w(1, "wv0", 0, D)))
                        ins.then_inc(full, 1)
                    elif kind == "b0":
                        pe.wait_ge(stack_step, stack_n.at(loop, ("qk0", phase, j, 0)))
                        s = scores.slot(step)
                        pe.wait_ge(sc_taken[s], scores.nth(loop, step))
                        t = i // 2
                        for q in range(QT):
                            for g in range(2):
                                r = slice(32 * (2 * (i % 2) + g), 32 * (2 * (i % 2) + g) + 32)
                                ins = pe.matmul(sc[s][:, g, q * TOK:(q + 1) * TOK], qs(j)[r, t, q * P:(q + 1) * P], ks(j)[r, t, :],
                                                start=True, stop=True, tile_position=(r.start, 0))
                        ins.then_inc(sc_full[s], 1)
                    elif kind == "m0":
                        pe.wait_ge(max_set, max_n.at(loop, ("b0", phase, j, 7)))
                        for k in range(2):
                            ps, full = free_tile(step, k)
                            for t in range(2):
                                for q in range(QT):
                                    a = (t * QT + q) * P
                                    ins = pe.transpose(ps[:, a:a + P], mx0(j)[:, q, 2 * k + t, :], ident[:])
                            ins.then_inc(full, 1)
                    elif kind == "c0":
                        if i == 0:
                            taken_tiles((("m0", phase, j, 0), 0), (("m0", phase, j, 0), 1))
                        s = scores.slot(step)
                        pe.wait_ge(sc_taken[s], scores.nth(loop, step))
                        t = i // 2
                        for q in range(QT):
                            for g in range(2):
                                r = slice(32 * (2 * (i % 2) + g), 32 * (2 * (i % 2) + g) + 32)
                                ins = pe.matmul(sc[s][:, g, q * TOK:(q + 1) * TOK], ks(j)[r, t, q * P:(q + 1) * P], qm(j)[r, t, :],
                                                start=True, stop=True, tile_position=(r.start, 0))
                        ins.then_inc(sc_full[s], 1)
                    elif kind == "pv0":
                        for c in (2 * i, 2 * i + 1):
                            e = ("c0", phase, j, c)
                            pe.wait_ge(sc_taken[scores.slot(e)], scores.taken(loop, e))
                        s = outs.slot(step)
                        if i % 2 == 0:
                            pe.wait_ge(ov_taken[s], outs.nth(loop, step))
                        if i == 0:
                            taken_tiles((("v0", phase, j, 0), 0))
                        for k in range(QT):
                            for g in range(4):
                                e = slot_of[("c0", phase, j, 2 * i + g // 2)]
                                a = ((g % 2) * QT + k) * TOK
                                ins = pe.matmul(ov[s][32 * g:32 * g + 32, (i % 2) * TOK:(i % 2 + 1) * TOK], v32(j)[:, k, 4 * i + g, :],
                                                probs[:, e, a:a + TOK], start=k == 0, stop=k == QT - 1, tile_position=(0, 32 * g))
                                if k == QT - 1 and g == 3 and i % 2 == 0:
                                    ins.then_inc(pv_done, 1)
                        if i % 2:
                            ins.then_inc(ov_full[s], 1)
                    elif kind == "o0":
                        values = [("pv0", phase, j, 2 * half + 1) if phase == "sa0" else ("pvc0", phase, j, half) for half in range(2)]
                        for slot, last in {outs.slot(st): st for st in values}.items():
                            pe.wait_ge(ov_taken[slot], outs.taken(loop, last))
                        for q in range(QT):
                            ps, full = free_tile(step, q)
                            for t in range(NT0):
                                ins = pe.transpose(ps[:, t * P:(t + 1) * P], oT0(j)[:, t * TOK + q * P:t * TOK + (q + 1) * P], ident[:])
                            ins.then_inc(full, 1)
                    elif kind == "oT":
                        ps, full = free_tile(step, after=[(("o0", phase, j, 0), k) for k in range(QT)])
                        for q in range(QT):
                            ins = pe.transpose(ps[:, q * P:(q + 1) * P], on[j][:, q * P:(q + 1) * P], ident[:])
                        ins.then_inc(full, 1)
                    elif kind == "wo":
                        after = []
                        if phase in ("sa0", "ca0"):
                            after = [(("oT", phase, j, 0), 0)]
                            name, n = ("wo0" if phase == "sa0" else "cwo0"), 1
                        elif phase in ("sa1", "ca1"):
                            after = [(("o1", phase, j, k), 0) for k in range(4)]
                            name, n = ("wo1" if phase == "sa1" else "wo2"), HP
                        else:
                            pe.wait_ge(g_step, g_n.at(loop, ("w1", phase, j, 0) if phase == "ff0" else ("wp", phase, j, 3)))
                            name, n = ("w2" if phase == "ff0" else "wf"), FF // P
                        ps, full = free_tile(step, after=after)
                        for k in range(n):
                            b = slice(k * TOK, (k + 1) * TOK)
                            ins = three(ps[:, 0:TOK], [w(m, name, k * P, (k + 1) * P) for m in range(2)], (qkh[j][:, b], qkl[j][:, b]),
                                        start=k == 0, stop=k == n - 1)
                        ins.then_inc(full, 1)
                    elif kind == "yT":
                        ps, full = free_tile(step, after=[(("wo", phase, j, 0), 0)])
                        for q in range(QT):
                            ins = pe.transpose(ps[:, q * P:(q + 1) * P], yT[j][:, q * P:(q + 1) * P], ident[:])
                        ins.then_inc(full, 1)
                    elif kind == "ck0":
                        pe.wait_ge(x_loaded[j], loop * 48 + 48)
                        ps, full = free_tile(step)
                        pe.matmul(ps[:, 0:KEYS], kv0[:, 0:D], ct[j][:, 0, :], start=True, stop=True)
                        pe.matmul(ps[:, KEYS:KEYS + D], ct[j][:].rearrange("c a k -> c (a k)"), kv0[:, D:2 * D],
                                  start=True, stop=True).then_inc(full, 1)
                    elif kind == "q0c":
                        pe.wait_ge(h_split, h_n.at(loop, ("hT", phase, j, 0)))
                        ps, full = free_tile(step)
                        three(ps[:, 0:TOK], [w(m, "cwq0", 0, D) for m in range(2)], (hh[j][:], hl[j][:])).then_inc(full, 1)
                    elif kind == "bc":
                        if phase == "ca0":
                            taken_tiles((("q0c", phase, j, 0), 0))
                            pe.wait_ge(kc_step, kc_n.at(loop, ("ck0", phase, j, 0)))
                        else:
                            pe.wait_ge(h_split, h_n.at(loop, ("hT", phase, j, 0)))
                            taken_tiles((("g1", phase, j, 0), 0), (("g1", phase, j, 0), 1))
                        s = scores.slot(step)
                        pe.wait_ge(sc_taken[s], scores.nth(loop, step))
                        q_hi = crossq(j, phase)[0]
                        for n in range(2):
                            ins = pe.matmul(sc[s][:, n, :], q_hi[:, i * P:(i + 1) * P], g_of(qkh, j)[:, n * BANK:(n + 1) * BANK],
                                            start=True, stop=True)
                        ins.then_inc(sc_full[s], 1)
                    elif kind == "mc":
                        pe.wait_ge(max_set, max_n.at(loop, step))
                        ps, full = free_tile(step)
                        for q in range(QT):
                            ins = pe.transpose(ps[:, 0:P].bitcast(BF16)[:, q * P:(q + 1) * P], mxc(j)[:, q, :], identb[:])
                        ins.then_inc(full, 1)
                    elif kind == "cc":
                        taken_tiles((("mc", phase, j, 0), 0))
                        s = scores.slot(step)
                        pe.wait_ge(sc_taken[s], scores.nth(loop, step))
                        for n in range(4):
                            pair = 4 * i + n
                            dst = sc[s][:, n // 2, (n % 2) * TOK:(n % 2 + 1) * TOK]
                            a = slice(pair * P, (pair + 1) * P)
                            qh_, ql_ = crossq(j, phase)
                            three(dst, (g_of(qkh, j)[:, a], g_of(qkl, j)[:, a]), (qh_[:, 0:TOK], ql_[:, 0:TOK]), stop=False)
                            ins = pe.matmul(dst, select[:, a], aug[j][:], start=False, stop=True)
                        ins.then_inc(sc_full[s], 1)
                    elif kind == "pvc0":
                        e = ("cc", phase, j, i)
                        pe.wait_ge(sc_taken[scores.slot(e)], scores.taken(loop, e))
                        if i == 0:
                            taken_tiles((("ck0", phase, j, 0), 0))
                        s = outs.slot(step)
                        pe.wait_ge(ov_taken[s], outs.nth(loop, step))
                        for n in range(4):
                            r = 64 * (n % 2)
                            ins = pe.matmul(ov[s][r:r + 64, (n // 2) * TOK:(n // 2 + 1) * TOK], vb0(j)[:, 4 * i + n, :],
                                            probs[:, slot_of[e], n * TOK:(n + 1) * TOK], start=True, stop=True, tile_position=(0, r))
                        ins.then_inc(ov_full[s], 1)
                    elif kind == "w1":
                        pe.wait_ge(h_split, h_n.at(loop, ("hT", phase, j, 0)))
                        for k in range(2):
                            ps, full = free_tile(step, k)
                            for t in range(2):
                                a = (2 * k + t) * P
                                ins = three(ps[:, t * TOK:(t + 1) * TOK], [w(m, "w1", a, a + P) for m in range(2)], (hh[j][:], hl[j][:]))
                            ins.then_inc(full, 1)
                    elif kind == "qk1":
                        pe.wait_ge(h_split, h_n.at(loop, ("hT", phase, j, 0)))
                        ps, full = free_tile(step)
                        for t, name in enumerate(("wq1", "wk1")):
                            ins = three(ps[:, t * TOK:(t + 1) * TOK], [w(m, name, i * P, (i + 1) * P) for m in range(2)], (hh[j][:], hl[j][:]))
                        ins.then_inc(full, 1)
                    elif kind == "v1":
                        ps, full = free_tile(step)
                        t, half = divmod(i, 2)
                        a = slice(t * P, (t + 1) * P)
                        three(ps[:], (hh[j][:, a], hl[j][:, a]), [w(m, "wv1", half * BANK, (half + 1) * BANK) for m in range(2)]).then_inc(full, 1)
                    elif kind == "b1":
                        taken_tiles((("qk1", phase, j, i), 0))
                        s = scores.slot(step)
                        pe.wait_ge(sc_taken[s], scores.nth(loop, step))
                        for q in range(QT):
                            for g in range(2):
                                r = slice(64 * g, 64 * g + 64)
                                ins = pe.matmul(sc[s][:, g, q * TOK:(q + 1) * TOK], qk(qkh, j, i, 0)[r, q * P:(q + 1) * P], qk(qkh, j, i, 1)[r, :],
                                                start=True, stop=True)
                        ins.then_inc(sc_full[s], 1)
                    elif kind == "c1":
                        taken_tiles((("mc", phase, j, 0), 0))
                        s = scores.slot(step)
                        pe.wait_ge(sc_taken[s], scores.nth(loop, step))
                        for t in range(QT):
                            keys = slice(t * P, (t + 1) * P)
                            for n, (kp, qp) in enumerate(((qkh, qkh), (qkh, qkl), (qkl, qkh))):
                                for g in range(2):
                                    r = slice(64 * g, 64 * g + 64)
                                    pe.matmul(sc[s][:, g, t * TOK:(t + 1) * TOK], qk(kp, j, i, 1)[r, keys], qk(qp, j, i, 0)[r, :],
                                              start=n == 0, stop=False)
                            for g in range(2):
                                r = slice(64 * g, 64 * g + 64)
                                ins = pe.matmul(sc[s][:, g, t * TOK:(t + 1) * TOK], select[r, i * P + 64 * g:i * P + 64 * g + 1].broadcast_to([64, P]),
                                                aug[j][r, :], start=False, stop=True)
                        ins.then_inc(sc_full[s], 1)
                    elif kind == "pv1":
                        e = ("c1", phase, j, i)
                        pe.wait_ge(sc_taken[scores.slot(e)], scores.taken(loop, e))
                        if i == 0:
                            pe.wait_ge(pool_set, pool_n.at(loop, ("v1", phase, j, 0)))
                            taken_tiles(*[(("v1", phase, j, n), 0) for n in range(4)])
                        s = outs.slot(step)
                        pe.wait_ge(ov_taken[s], outs.nth(loop, step))
                        for g in range(2):
                            for q in range(QT):
                                for k in range(QT):
                                    a = (g * QT + k) * TOK + q * P
                                    ins = pe.matmul(ov[s][:, (g * QT + q) * 65:(g * QT + q + 1) * 65], probs[:, slot_of[e], a:a + P],
                                                    v65(j)[:, k, 2 * i + g, :], start=k == 0, stop=k == QT - 1)
                        ins.then_inc(ov_full[s], 1)
                    elif kind == "pvc1":
                        e = ("cc", phase, j, i // 4)
                        if i % 4 == 0:
                            pe.wait_ge(sc_taken[scores.slot(e)], scores.taken(loop, e))
                        if i == 0:
                            taken_tiles((("cv1", phase, j, 0), 0), (("cv1", phase, j, 0), 1))
                        s = outs.slot(step)
                        pe.wait_ge(ov_taken[s], outs.nth(loop, step))
                        for q in range(QT):
                            a = (i % 4) * TOK + q * P
                            ins = pe.matmul(ov[s][:, q * 130:(q + 1) * 130], probs[:, slot_of[e], a:a + P], vb1(j)[:, i, :], start=True, stop=True)
                        ins.then_inc(ov_full[s], 1)
                    elif kind == "o1":
                        if i == 0:
                            values = [("pv1" if phase == "sa1" else "pvc1", phase, j, k) for k in range(HP)]
                            for slot, last in {outs.slot(st): st for st in values}.items():
                                pe.wait_ge(ov_taken[slot], outs.taken(loop, last))
                        ps, full = free_tile(step)
                        for t in range(2):
                            for q in range(QT):
                                a, b = q * 1024 + (2 * i + t) * P, (t * QT + q) * P
                                ins = pe.transpose(ps[:, b:b + P], on[j][:, a:a + P], ident[:])
                        ins.then_inc(full, 1)
                    elif kind == "ck1":
                        ps, full = free_tile(step)
                        for k in range(HP):
                            ins = pe.matmul(ps[:, k * KEYS:(k + 1) * KEYS], kv1[0:CTX, 0, k * P:(k + 1) * P], ct[j][:, 0, :], start=True, stop=True)
                        ins.then_inc(full, 1)
                    elif kind == "g1":
                        for k in range(2):
                            ps, full = free_tile(step, k, after=[(("ck1", phase, j, 0), 0)])
                            for n in range(4):
                                a = slice((4 * k + n) * P, (4 * k + n + 1) * P)
                                ins = pe.matmul(ps[:, n * P:(n + 1) * P], kv1[:, 2, a], on[j][:, a], start=True, stop=True)
                            ins.then_inc(full, 1)
                    elif kind == "cv1":
                        for k in range(2):
                            ps, full = free_tile(step, k)
                            pe.matmul(ps[:], ct[j][:].rearrange("c a k -> c (a k)"), kv1[0:CTX, 1, k * BANK:(k + 1) * BANK],
                                      start=True, stop=True).then_inc(full, 1)
                    elif kind == "wp":
                        pe.wait_ge(h_split, h_n.at(loop, ("hT", phase, j, 0)))
                        ps, full = free_tile(step)
                        for t in range(2):
                            a = t * FF + i * P
                            ins = three(ps[:, t * TOK:(t + 1) * TOK], [w(m, "wp", a, a + P) for m in range(2)], (hh[j][:], hl[j][:]))
                        ins.then_inc(full, 1)


def kernel(**inputs):
    import concourse.bacc as bacc
    from concourse.bass_utils import run_bass_kernel_spmd

    a = {k: np.asarray(t) for k, t in inputs.items()}

    def turned(name):
        return np.ascontiguousarray(a[name].T)

    def by_rows(m, out_cols=None):
        n = m.shape[0] // P
        return m.reshape(n, P, -1).transpose(1, 0, 2).reshape(P, -1)

    def four_times(m):
        return np.repeat(m.reshape(P, H, 1, HD0), 4, axis=2).reshape(P, 4 * P)

    w0 = np.concatenate([four_times(turned("L0_xattn_sa_wq")), four_times(turned("L0_xattn_sa_wk")), turned("L0_xattn_sa_wv"), turned("L0_xattn_sa_wo"),
                         turned("L0_xattn_ca_wq"), turned("L0_xattn_ca_wo"), turned("L0_xattn_mlp_w1"),
                         by_rows(turned("L0_xattn_mlp_w2"))], axis=1)
    w1 = np.concatenate([a["L1_xattn_Wq1"], a["L1_xattn_Wk1"], a["L1_xattn_Wv1"], by_rows(a["L1_xattn_Wo1"]), by_rows(a["L1_xattn_Wo2"]),
                         a["L1_xattn_Wp"], by_rows(a["L1_xattn_Wf"])], axis=1)
    kv0 = np.concatenate([turned("L0_xattn_ca_wk"), turned("L0_xattn_ca_wv")], axis=1)
    kv1 = np.zeros((P, 3, 1024), np.float32)
    kv1[:CTX, 0], kv1[:CTX, 1], kv1[:, 2] = a["L1_xattn_Wk2"], a["L1_xattn_Wv2"], by_rows(turned("L1_xattn_Wq2"))

    def stacked(bias, one):
        b = bias.reshape(NT0, 4, 1, HD0)
        rest = np.zeros((NT0, 4, 1, HD0), np.float32)
        rest[..., 0] = one
        return np.concatenate([b, b, b, rest], axis=2).reshape(NT0, P).T

    row = np.arange(P)
    part = (row % 32) // HD0
    cols = lambda name: a[name].reshape(-1, P).T
    vec = {"bqs": stacked(a["L0_xattn_sa_bq"], 0), "bks": stacked(a["L0_xattn_sa_bk"], 1),
           "cbq": cols("L0_xattn_ca_bq"), "cbk": cols("L0_xattn_ca_bk"), "bo0": cols("L0_xattn_sa_bo"), "cbo0": cols("L0_xattn_ca_bo"),
           "b1m": cols("L0_xattn_mlp_b1"), "b2m": cols("L0_xattn_mlp_b2"), "bo1": cols("L1_xattn_bo1"), "bo2": cols("L1_xattn_bo2"),
           "bp": cols("L1_xattn_bp"), "bf": cols("L1_xattn_bf"),
           "keep": (part < 3).astype(np.float32)[:, None], "subq": -(part == 1).astype(np.float32)[:, None],
           "subk": -(part == 2).astype(np.float32)[:, None],
           "mask": (row[:, None] // HD0 == np.arange(H)).astype(np.float32)}
    for n, (g, b) in enumerate([(f"L{l}_xattn_{g}{k}{e}", f"L{l}_xattn_{b}{k}{f}") for l, g, b, e, f in ((0, "ln", "ln", "_g", "_b"), (1, "g", "b", "", ""))
                                for k in (1, 2, 3)]):
        vec[f"g{n}"], vec[f"b{n}"] = cols(g), cols(b)
    vec = np.ascontiguousarray(np.concatenate([vec[name] for name in VEC_NAMES], axis=1))
    assert vec.shape[1] == VEC_N and w0.shape[1] == W0_N and w1.shape[1] == W1_N
    pair, col = np.arange(HP * P) // P, np.arange(HP * P) % P
    r = row[:, None]
    select = ((r // 64 == col // 64) & (r % 64 < 2 * HP) & (r % HP == pair)).astype(np.float32)
    arrays = {"x_in": a["x"], "ctx_in": np.ascontiguousarray(a["ctx_768"].transpose(0, 2, 1)), "w0_in": np.ascontiguousarray(w0), "w1_in": np.ascontiguousarray(w1),
              "kv0_in": np.ascontiguousarray(kv0), "kv1_in": kv1.reshape(P, -1), "vec_in": vec,
              "bv_in": np.concatenate([a["L0_xattn_sa_bv"], a["L0_xattn_ca_bv"]]), "id_in": np.eye(P, dtype=np.float32), "sel_in": select}
    nc = bacc.Bacc("TRN2", target_bir_lowering=False, num_devices=1)
    args = [nc.dram_tensor(k, t.shape, F32, kind="ExternalInput").ap() for k, t in arrays.items()]
    out = nc.dram_tensor("out", (BATCH, TOK, D), F32, kind="ExternalOutput").ap()
    build(nc, *args, out)
    r = run_bass_kernel_spmd(nc, [arrays], core_ids=[0])
    return r.results[0]["out"]
```

```python
from contextlib import ExitStack

import numpy as np

import concourse.bass as bass
import concourse.mybir as mybir

F32 = mybir.dt.float32
F32R = mybir.dt.float32r
BF16 = mybir.dt.bfloat16
ACT = mybir.ActivationFunctionType
ALU = mybir.AluOpType
AX_X = mybir.AxisListType.X

P = 128
BATCH, TOK, D = 4, 256, 128
KEYS, CTX = 64, 96
NE = 3
H = 16
HD0, HD1 = 8, 64
FF = 512
QT = TOK // P
PAIR = 2
LOOPS = BATCH // PAIR
HP = H // 2
NT0 = H // 4
EPS = 1e-5
SCALE0, SCALE1 = HD0 ** -0.5, HD1 ** -0.5
BANK = 512
HALF = 2 * BANK

W0_NAMES = ["wq0", "wk0", "wv0", "wo0", "cwq0", "cwo0", "w1", "w2"]
W0_COLS = dict(zip(W0_NAMES, [4 * P, 4 * P] + [P] * 4 + [FF, FF]))
W1_NAMES = ["wq1", "wk1", "wv1", "wo1", "wo2", "wp", "wf"]
W1_COLS = dict(zip(W1_NAMES, [1024] * 5 + [2 * FF, FF]))
VEC_NAMES = ["g0", "g1", "g2", "g3", "g4", "g5", "b0", "b1", "b2", "b3", "b4", "b5",
             "bqs", "bks", "cbq", "cbk", "bo0", "cbo0", "b1m", "b2m", "bo1", "bo2", "bp", "bf",
             "subq", "subk", "mask", "half"]
VEC_COLS = dict(zip(VEC_NAMES, [1] * 12 + [4, 4] + [1] * 4 + [4, 1, 1, 1, 8, 1] + [1, 1, H, QT]))


def offsets(cols):
    out, at = {}, 0
    for name, n in cols.items():
        out[name] = at
        at += n
    return out, at


VEC_AT, VEC_N = offsets(VEC_COLS)
W0_AT, W0_N = offsets(W0_COLS)
W1_AT, W1_N = offsets(W1_COLS)


PHASES = ["sa0", "ca0", "ff0", "sa1", "ca1", "ff1"]


ORDER = """
A.sa0 ln B.sa0 ln A.sa0 nm B.sa0 nm hT A.sa0 hT B.sa0 v0 A.sa0 qk0 v0 B.sa0 qk0 A.sa0 b0 b0 b0 b0 B.sa0 b0
A.sa0 b0 b0 B.sa0 b0 A.sa0 b0 b0 B.sa0 b0 b0 b0 b0 b0 A.sa0 m0 B.sa0 b0 A.sa0 c0 c0 c0 B.sa0 m0 A.sa0 pv0 c0
c0 pv0 c0 c0 pv0 c0 B.sa0 c0 A.sa0 pv0 B.sa0 c0 c0 A.sa0 o0 B.sa0 pv0 c0 c0 A.ca0 ck0 B.sa0 pv0 c0 c0 pv0 c0
A.sa0 oT B.sa0 pv0 A.sa0 wo B.sa0 o0 A.sa0 yT B.ca0 ck0 A.ca0 ln nm B.sa0 oT A.ca0 hT B.sa0 wo yT A.ca0 q0c
B.ca0 ln A.ca0 bc bc B.ca0 nm A.ca0 mc B.ca0 hT A.ca0 cc B.ca0 q0c A.ca0 cc pvc0 B.ca0 bc bc A.ca0 pvc0 o0
B.ca0 mc A.ca0 oT B.ca0 cc A.ca0 wo B.ca0 cc A.ca0 yT B.ca0 pvc0 pvc0 A.ff0 ln B.ca0 o0 A.ff0 nm B.ca0 oT
A.ff0 hT B.ca0 wo yT A.ff0 w1 B.ff0 ln nm A.ff0 wo B.ff0 hT A.ff0 yT A.sa1 ln B.ff0 w1 A.sa1 nm B.ff0 wo A.sa1
hT B.ff0 yT A.sa1 qk1 B.sa1 ln A.sa1 qk1 qk1 b1 B.sa1 nm A.sa1 qk1 b1 b1 qk1 v1 v1 B.sa1 hT A.sa1 qk1 qk1 qk1
v1 v1 b1 B.sa1 v1 v1 A.sa1 b1 b1 b1 b1 B.sa1 qk1 v1 v1 qk1 qk1 qk1 A.sa1 mc B.sa1 qk1 qk1 b1 qk1 A.sa1 c1 c1
B.sa1 b1 b1 A.sa1 pv1 B.sa1 b1 b1 b1 A.sa1 pv1 B.sa1 qk1 b1 A.sa1 c1 c1 pv1 B.sa1 b1 A.sa1 c1 c1 B.sa1 mc
A.sa1 pv1 pv1 B.sa1 c1 A.sa1 pv1 B.sa1 pv1 c1 c1 pv1 pv1 c1 c1 pv1 c1 c1 pv1 pv1 A.sa1 c1 B.sa1 pv1 A.sa1 pv1
c1 B.sa1 c1 A.sa1 pv1 B.sa1 pv1 A.sa1 o1 A.ca1 cv1 A.sa1 o1 o1 o1 B.sa1 o1 o1 o1 o1 B.ca1 cv1 A.ca1 ck1 A.sa1
wo B.sa1 wo B.ca1 ck1 A.sa1 yT B.sa1 yT A.ca1 g1 B.ca1 ln g1 A.ca1 ln B.ca1 nm A.ca1 nm B.ca1 hT A.ca1 hT
B.ca1 bc bc A.ca1 bc bc B.ca1 mc cc cc pvc1 pvc1 A.ca1 mc B.ca1 pvc1 pvc1 A.ca1 cc cc pvc1 B.ca1 pvc1 A.ca1
pvc1 pvc1 B.ca1 pvc1 A.ca1 pvc1 pvc1 B.ca1 pvc1 pvc1 A.ca1 pvc1 pvc1 pvc1 B.ca1 o1 o1 o1 o1 A.ca1 o1 o1 o1 o1
B.ca1 wo A.ca1 wo B.ca1 yT A.ca1 yT B.ff1 ln A.ff1 ln B.ff1 nm A.ff1 nm B.ff1 hT A.ff1 hT B.ff1 wp A.ff1 wp wp
wp wp B.ff1 wp wp wp A.ff1 wo yT B.ff1 wo yT
"""


def schedule():
    out, counts = [], {}
    for token in ORDER.split():
        if "." in token:
            j, phase = "AB".index(token[0]), token[2:]
        else:
            i = counts.get((token, phase, j), 0)
            counts[token, phase, j] = i + 1
            out.append((token, phase, j, i))
    return out


SCHEDULE = schedule()
EXPS = ("c0", "c1", "cc")


def reader(step):
    kind, phase, j, c = step
    if kind == "c0":
        return "pv0", phase, j, c // 2
    if kind == "c1":
        return "pv1", phase, j, c
    return ("pvc0", phase, j, c) if phase == "ca0" else ("pvc1", phase, j, 4 * c + 3)


def slots_free(order):
    exps = [s for s in order if s[0] in EXPS]
    return all(order.index(reader(old)) < order.index(new) for old, new in zip(exps, exps[NE:]))


assert slots_free(SCHEDULE)


def count_of(uses, step):
    n = uses.get(step[0], 0)
    return n(step) if callable(n) else n


class Tally:

    def __init__(self, **incs):
        self.start, self.incs, n = {}, incs, 0
        for s in SCHEDULE:
            self.start[s] = n
            n += count_of(incs, s)
        self.total = n

    def at(self, loop, step, k=None):
        k = count_of(self.incs, step) if k is None else k
        return loop * self.total + (self.start[step] + k)


class Ring:

    def __init__(self, size, **uses):
        self.size, self.per_slot, self.use = size, [0] * size, {}
        n = 0
        for s in SCHEDULE:
            for k in range(count_of(uses, s)):
                slot = n % size
                self.per_slot[slot] += 1
                self.use[s, k] = (slot, self.per_slot[slot])
                n += 1

    def slot(self, step, k=0):
        return self.use[step, k][0]

    def nth(self, loop, step, k=0):
        slot, n = self.use[step, k]
        return loop * self.per_slot[slot] + n

    def taken(self, loop, step, k=0):
        slot, n = self.use[step, k]
        return loop * self.per_slot[slot] + (n + 1)


def build(nc, x_in, ctx_in, w0_in, w1_in, kv0_in, kv1_in, vec_in, bv_in, id_in, sel_in, out):
    ln_n = Tally(ln=5, nm=2)
    rstd_n = Tally(ln=1)
    h_n = Tally(hT=2)
    hi_n = Tally(qk0=4, oT=1, o1=1, q0c=1, qk1=1, g1=2, wp=1)
    pool_n = Tally(v0=2, qk0=1, hT=lambda s: s[1] in ("ca0", "sa1", "ca1"), v1=lambda s: s[3] == 0,
                   ck0=5, ck1=1, cv1=3)
    max_n = Tally(mc=2)
    norm_n = Tally(o0=2, pv1=1, pvc1=1)
    g_n = Tally(w1=4, wp=2)
    kc_n = Tally(ck0=4)
    banks = Ring(8, hT=1, qk0=4, v0=1, m0=2, o0=2, oT=1, wo=1, yT=1, ck0=1, q0c=1, mc=1, w1=2,
                 qk1=1, v1=1, o1=1, ck1=1, g1=2, cv1=2, wp=1,
                 b0=2, c0=2, b1=2, c1=2, bc=2, cc=2, pv1=1, pvc1=1, pvc0=1, pv0=lambda s: s[3] % 2 == 0)
    slot_of = {s: n % NE for n, s in enumerate(s for s in SCHEDULE if s[0] in EXPS)}

    ctx = ExitStack()
    with ctx:
        def sb(name, shape, dt=F32):
            return ctx.enter_context(nc.sbuf_tensor(name, shape, dt))

        def sem(name):
            return ctx.enter_context(nc.semaphore(name))

        w0h, w0l = sb("w0h", [P, W0_N], F32R), sb("w0l", [P, W0_N], F32R)
        w1h, w1l = sb("w1h", [P, W1_N], F32R), sb("w1l", [P, W1_N], F32R)
        kv0 = sb("kv0", [CTX, 2 * D])
        kv1 = sb("kv1", [P, 3, 1024])
        vec = sb("vec", [P, VEC_N])
        bv = sb("bv", [P, 2, D])
        ident = sb("ident", [P, P])
        select = sb("select", [P, HP * P], BF16)
        identb = sb("identb", [P, P], BF16)
        minus_bias = sb("minus_bias", [P, 2 * NT0])
        x = [sb(f"x{j}", [P, QT, D]) for j in range(PAIR)]
        yT = [sb(f"yT{j}", [P, TOK]) for j in range(PAIR)]
        hh = [sb(f"hh{j}", [P, TOK], F32R) for j in range(PAIR)]
        hl = [sb(f"hl{j}", [P, TOK], F32R) for j in range(PAIR)]
        aug = [sb(f"aug{j}", [P, TOK], BF16) for j in range(PAIR)]
        qkh = [sb(f"qkh{j}", [P, 4096], F32R) for j in range(PAIR)]
        qkl = [sb(f"qkl{j}", [P, 4096], F32R) for j in range(PAIR)]
        vv = [sb(f"vv{j}", [P, QT * H * (HD1 + 1)]) for j in range(PAIR)]
        on = [sb(f"on{j}", [P, QT * H * HD1]) for j in range(PAIR)]
        ct = [sb(f"ct{j}", [CTX, 2, KEYS]) for j in range(PAIR)]
        stats = [sb(f"stats{j}", [P, QT, 6]) for j in range(PAIR)]
        mv = [sb(f"mv{j}", [P, QT, 2]) for j in range(PAIR)]
        ve = [sb(f"ve{j}", [P, QT]) for j in range(PAIR)]
        rstd = [sb(f"rstd{j}", [P, QT]) for j in range(PAIR)]
        rden = [sb(f"rden{j}", [P, QT * H]) for j in range(PAIR)]
        probs = sb("probs", [P, NE, HALF])

        bank = [ctx.enter_context(nc.psum_tensor(f"bank{i}", [P, BANK], F32)) for i in range(8)]

        x_loaded = [sem(f"x_loaded{j}") for j in range(PAIR)]
        ctx_loaded = [sem(f"ctx_loaded{j}") for j in range(PAIR)]
        x_used = [sem(f"x_used{j}") for j in range(PAIR)]
        ctx_used = [sem(f"ctx_used{j}") for j in range(PAIR)]
        w0_loaded, w1_loaded, wn_loaded, small_loaded = sem("w0_loaded"), sem("w1_loaded"), sem("wn_loaded"), sem("small_loaded")
        w0_hi, w0_lo, w1_hi, w1_lo = sem("w0_hi"), sem("w0_lo"), sem("w1_hi"), sem("w1_lo")
        pool_passed, dve_passed = sem("pool_passed"), sem("dve_passed")
        stored = [sem(f"stored{j}") for j in range(PAIR)]
        bank_full = [sem(f"bank_full{i}") for i in range(8)]
        bank_taken = [sem(f"bank_taken{i}") for i in range(8)]
        ln_step = sem("ln_step")
        rstd_set = sem("rstd_set")
        h_split = sem("h_split")
        hi_set = sem("hi_set")
        pool_set = sem("pool_set")
        max_set = sem("max_set")
        norm_step = sem("norm_step")
        g_step = sem("g_step")
        kc_step = sem("kc_step")

        def v(name, i=0, n=1):
            at = VEC_AT[name] + i
            return vec[:, at:at + n]

        def w(hi_lo, name, a, b):
            tile, at = ((w0h, w0l), W0_AT) if name in W0_AT else ((w1h, w1l), W1_AT)
            return tile[hi_lo][:, at[name] + a:at[name] + b]

        def qs(j):
            return qkh[j][:, 0:1024].rearrange("p (t q) -> p t q", t=NT0)

        def qm(j):
            return qkh[j][:, 1024:2048].rearrange("p (t q) -> p t q", t=NT0)

        def ks(j):
            return qkh[j][:, 2048:3072].rearrange("p (t q) -> p t q", t=NT0)

        def qk(tile, j, jj, which):
            a = (jj * 2 + which) * TOK
            return tile[j][:, a:a + TOK]

        def g_of(tile, j):
            return tile[j][:, 2048:3072]

        def v32(j):
            return vv[j][:, 0:1024].rearrange("p (t h c) -> p t h c", t=QT, h=H)

        def v65(j):
            return vv[j][:, :].rearrange("p (t h c) -> p t h c", t=QT, h=H)

        def vb0(j):
            return vv[j][:, 0:512].rearrange("p (w c) -> p w c", w=HP)

        def vb1(j):
            return vv[j][:, 0:HP * 130].rearrange("p (w c) -> p w c", w=HP)

        def mx0(j):
            return on[j][:, 0:1024].rearrange("p (t n c) -> p t n c", t=QT, n=NT0)

        def mxc(j):
            return on[j][:, 0:P].bitcast(BF16).rearrange("p (t c) -> p t c", t=QT)

        def xin(j):
            return vv[j][:, 1792:1792 + QT * D].rearrange("p (t d) -> p t d", t=QT)

        def tokens(j, phase):
            return xin(j) if phase == "sa0" else x[j]

        def raw_max(j):
            return rden[j][:].rearrange("p (t g w) -> p t g w", t=QT, g=2)

        def oT0(j):
            return on[j][:, 1024:2048]

        def crossq(j, phase):
            return (qkh[j][:, 0:TOK], qkl[j][:, 0:TOK]) if phase == "ca0" else (hh[j], hl[j])

        def spread(ap, n):
            return ap.unsqueeze(len(ap.shape)).broadcast_to([*ap.shape, n])

        raw0 = probs[:].rearrange("p e n -> p (e n)")[:, 0:W0_N]
        raw1 = [on[1][:], vv[1][:, 0:1792], on[0][:], vv[0][:, 1024:1792]]
        raw1_at = [0, 2048, 3840, 5888]

        block = ctx.enter_context(nc.Block())

        @block.sync
        def _(sp):
            sp.dma_start(vec[:], vec_in).then_inc(small_loaded, 16)
            sp.dma_start(ident[:], id_in).then_inc(small_loaded, 16)
            sp.dma_start(bv[:].rearrange("p a d -> p (a d)"), bv_in.partition_broadcast(P)).then_inc(small_loaded, 16)
            sp.dma_start(vv[0][:, 0:HP * P], sel_in).then_inc(small_loaded, 16)
            for j in range(PAIR):
                sp.sem_inc(x_used[j], 1)
                sp.sem_inc(ctx_used[j], 1)
            with sp.Fori(0, LOOPS) as loop:
                for j in range(PAIR):
                    sp.wait_ge(x_used[j], loop + 1)
                    sp.dma_start(xin(j), x_in[loop * PAIR + j].rearrange("(t p) d -> p t d", p=P)).then_inc(x_loaded[j], 16)
                for j in range(PAIR):
                    sp.wait_ge(ctx_used[j], loop + 1)
                    for twice in range(2):
                        sp.dma_start(ct[j][:, twice, :], ctx_in[loop * PAIR + j]).then_inc(ctx_loaded[j], 16)
            for j in range(PAIR):
                sp.wait_ge(stored[j], 16 * LOOPS + 16)

        @block.scalar
        def _(act):
            act.dma_start(raw0, w0_in).then_inc(w0_loaded, 16)
            act.dma_start(kv0[:], kv0_in).then_inc(wn_loaded, 16)
            for raw, at in zip(raw1, raw1_at):
                act.dma_start(raw, w1_in[:, at:at + raw.shape[1]]).then_inc(w1_loaded, 16)
            act.dma_start(kv1[:].rearrange("p a n -> p (a n)"), kv1_in).then_inc(wn_loaded, 16)
            act.wait_ge(w0_loaded, 16)
            act.activation(w0h[:], raw0, ACT.Copy).then_inc(w0_hi, 1)
            act.wait_ge(small_loaded, 64)
            act.activation(select[:], vv[0][:, 0:HP * P], ACT.Copy).then_inc(w0_hi, 1)
            act.wait_ge(w1_loaded, 64)
            for raw, at in zip(raw1, raw1_at):
                act.activation(w1h[:, at:at + raw.shape[1]], raw, ACT.Copy).then_inc(w1_hi, 1)
            for s in stored:
                act.sem_inc(s, 16)
            act.wait_ge(w0_lo, 4)
            act.wait_ge(w1_lo, 4)
            with act.Fori(0, LOOPS) as loop:
                def full_tile(step, k=0):
                    s = banks.slot(step, k)
                    act.wait_ge(bank_full[s], banks.nth(loop, step, k))
                    return bank[s], bank_taken[s]

                for step in SCHEDULE:
                    kind, phase, j, i = step
                    if kind == "hT":
                        n = PHASES.index(phase)
                        ps, taken = full_tile(step)
                        act.activation(yT[j][:], ps[:, 0:TOK], ACT.Identity, bias=v(f"b{n}"), scale=v(f"g{n}")).then_inc(taken, 1)
                    elif kind == "qk0":
                        for k in range(4):
                            ps, _ = full_tile(step, k)
                            for t in range(2):
                                n = (0 if k < 2 else NT0) + 2 * (k % 2) + t
                                ins = act.activation(qkl[j][:, k * BANK + t * TOK:k * BANK + (t + 1) * TOK], ps[:, t * TOK:(t + 1) * TOK], ACT.Identity,
                                                     bias=minus_bias[:, n:n + 1], scale=v("subq" if k < 2 else "subk"))
                            ins.then_inc(hi_set, 1)
                    elif kind in ("c0", "c1", "cc"):
                        for k in range(2):
                            ps, taken = full_tile(step, k)
                            act.activation(probs[:, slot_of[step], k * BANK:(k + 1) * BANK], ps[:], ACT.Exp,
                                           scale=SCALE0 if phase in ("sa0", "ca0") else SCALE1).then_inc(taken, 1)
                    elif (kind == "pv0" and i % 2) or kind == "pvc0":
                        use, half = (("pv0", phase, j, i - 1), i // 2) if kind == "pv0" else (step, i)
                        ps, taken = full_tile(use)
                        act.activation(oT0(j)[:, half * BANK:(half + 1) * BANK], ps[:], ACT.Copy).then_inc(taken, 1)
                    elif kind == "v1":
                        ps, taken = full_tile(step)
                        t, half = divmod(i, 2)
                        act.activation(v65(j)[:, t, half * 8:half * 8 + 8, 0:HD1], ps[:].rearrange("p (h d) -> p h d", h=8), ACT.Copy).then_inc(taken, 1)
                    elif kind == "ck1":
                        act.wait_ge(pool_set, pool_n.at(loop, step))
                        ps, taken = full_tile(step)
                        dst = on[j][:, 0:1024].rearrange("p (w c) -> p w c", w=HP)
                        src = ps[:].rearrange("p (w k) -> p w k", w=HP)
                        act.activation(dst[0:KEYS, :, 0:KEYS], src[0:KEYS], ACT.Copy)
                        act.activation(dst[KEYS:P, :, KEYS:P], src[KEYS:P], ACT.Copy).then_inc(taken, 1)
                    elif kind == "cv1":
                        for k in range(2):
                            if k == 0:
                                act.wait_ge(pool_set, pool_n.at(loop, step))
                            ps, taken = full_tile(step, k)
                            src = ps[:].rearrange("p (w g d) -> p w g d", g=2, d=HD1)
                            dst = vb1(j)[:, 4 * k:4 * k + 4, :]
                            act.activation(dst[0:KEYS, :, 0:HD1], src[0:KEYS, :, 0, :], ACT.Copy)
                            act.activation(dst[KEYS:P, :, 65:65 + HD1], src[KEYS:P, :, 1, :], ACT.Copy).then_inc(taken, 1)
                    elif kind == "mc":
                        ps, taken = full_tile(step)
                        act.activation(aug[j][:], ps[:, 0:P].bitcast(BF16), ACT.Copy).then_inc(taken, 1)
                    elif kind in ("oT", "q0c"):
                        ps, _ = full_tile(step)
                        bias = v("cbq") if kind == "q0c" else 0.0
                        act.activation(qkh[j][:, 0:TOK], ps[:, 0:TOK], ACT.Identity, bias=bias).then_inc(hi_set, 1)
                    elif kind in ("qk1", "o1"):
                        ps, _ = full_tile(step)
                        act.activation(qkh[j][:, i * BANK:(i + 1) * BANK], ps[:], ACT.Copy).then_inc(hi_set, 1)
                    elif kind == "g1":
                        for k in range(2):
                            ps, _ = full_tile(step, k)
                            act.activation(g_of(qkh, j)[:, k * BANK:(k + 1) * BANK], ps[:], ACT.Copy).then_inc(hi_set, 1)
                    elif kind == "w1":
                        for k in range(2):
                            ps, taken = full_tile(step, k)
                            for t in range(2):
                                ins = act.activation(on[j][:, k * BANK + t * TOK:k * BANK + (t + 1) * TOK], ps[:, t * TOK:(t + 1) * TOK], ACT.Gelu,
                                                     bias=v("b1m", 2 * k + t))
                            ins.then_inc(taken, 1)
                    elif kind == "wp":
                        ps, _ = full_tile(step)
                        act.activation(on[j][:, 1024 + i * TOK:1024 + (i + 1) * TOK], ps[:, TOK:2 * TOK], ACT.Gelu, bias=v("bp", 4 + i)).then_inc(hi_set, 1)
                    elif kind == "yT" and phase == "ff1":
                        act.wait_ge(bank_taken[banks.slot(step)], banks.taken(loop, step))
                        act.dma_start(out[loop * PAIR + j].rearrange("(t p) d -> p t d", p=P), x[j][:]).then_inc(stored[j], 16)
                    elif kind == "wo":
                        ps, taken = full_tile(step)
                        bias = {"sa0": "bo0", "ca0": "cbo0", "ff0": "b2m", "sa1": "bo1", "ca1": "bo2", "ff1": "bf"}[phase]
                        act.activation(yT[j][:], ps[:, 0:TOK], ACT.Identity, bias=v(bias)).then_inc(taken, 1)

        @block.gpsimd
        def _(pool):
            pool.wait_ge(small_loaded, 64)
            pool.wait_ge(w1_hi, 4)
            pool.wait_ge(w1_lo, 4)
            pool.wait_ge(w0_hi, 2)
            with pool.Fori(0, LOOPS) as loop:
                for step in SCHEDULE:
                    kind, phase, j, i = step

                    def settled():
                        pool.sem_inc(pool_passed, 1)

                    def behind(k=0):
                        s = banks.slot(step, k)
                        pool.wait_ge(bank_full[s], banks.nth(loop, step, k))
                        settled()

                    if kind == "ln":
                        pool.wait_ge(ln_step, ln_n.at(loop, step, 5))
                        pool.tensor_tensor(rstd[j][:], ve[j][:], v("half", 0, QT), ALU.pow).then_inc(rstd_set, 1)
                    elif kind == "hT" and count_of(pool_n.incs, step):
                        behind()
                        pool.memset(on[j][:, 0:P], 0.0).then_inc(pool_set, 1)
                    elif kind == "qk0":
                        behind()
                        pool.memset(on[j][:, 0:1024], 0.0).then_inc(pool_set, 1)
                    elif kind == "v0":
                        behind()
                        pool.memset(vv[j][:, 0:1024], 0.0).then_inc(pool_set, 1)
                        pool.wait_ge(pool_set, pool_n.at(loop, step, 1))
                        settled()
                        pool.memset(v32(j)[:, :, :, HD0:HD0 + 1], 1.0).then_inc(pool_set, 1)
                    elif kind == "v1" and i == 0:
                        behind()
                        pool.memset(v65(j)[:, :, :, HD1:HD1 + 1], 1.0).then_inc(pool_set, 1)
                    elif kind == "ck0":
                        behind()
                        pool.memset(vv[j][:, 0:512], 0.0).then_inc(pool_set, 1)
                        pool.wait_ge(pool_set, pool_n.at(loop, step, 1))
                        settled()
                        pool.memset(vb0(j)[0:KEYS, :, 8:9], 1.0).then_inc(pool_set, 1)
                        pool.memset(vb0(j)[KEYS:P, :, 40:41], 1.0).then_inc(pool_set, 1)
                        pool.wait_ge(pool_set, pool_n.at(loop, step, 3))
                        pool.wait_ge(kc_step, kc_n.at(loop, step, 3))
                        mask = spread(v("mask", 0, H), KEYS)
                        for part, dst in ((hh[j][:, 0:KEYS].bitcast(F32), g_of(qkh, j)), (hl[j][:, 0:KEYS].bitcast(F32), g_of(qkl, j))):
                            pool.tensor_tensor(dst.rearrange("p (h k) -> p h k", h=H), part.unsqueeze(1).broadcast_to([P, H, KEYS]), mask,
                                               ALU.mult).then_inc(pool_set, 1)
                    elif kind == "ck1":
                        behind()
                        pool.memset(on[j][:, 0:1024], 0.0).then_inc(pool_set, 1)
                    elif kind == "cv1":
                        behind()
                        pool.memset(vv[j][:, 0:HP * 130], 0.0).then_inc(pool_set, 1)
                        pool.wait_ge(pool_set, pool_n.at(loop, step, 1))
                        settled()
                        pool.memset(vb1(j)[0:KEYS, :, 64:65], 1.0).then_inc(pool_set, 1)
                        pool.memset(vb1(j)[KEYS:P, :, 129:130], 1.0).then_inc(pool_set, 1)
                        pool.wait_ge(pool_set, pool_n.at(loop, step, 3))
                        settled()

        @block.vector
        def _(dve):
            dve.wait_ge(w0_loaded, 16)
            dve.wait_ge(w0_hi, 1)
            dve.tensor_tensor(w0l[:], raw0, w0h[:].bitcast(F32), ALU.subtract).then_inc(w0_lo, 1)
            for k, (raw, at) in enumerate(zip(raw1, raw1_at)):
                dve.wait_ge(w1_hi, k + 1)
                cols = slice(at, at + raw.shape[1])
                dve.tensor_tensor(w1l[:, cols], raw, w1h[:, cols].bitcast(F32), ALU.subtract).then_inc(w1_lo, 1)
            dve.wait_ge(small_loaded, 64)
            dve.tensor_copy(identb[:], ident[:]).then_inc(w0_lo, 1)
            for k, (bias, sub) in enumerate((("bqs", "subq"), ("bks", "subk"))):
                dve.tensor_scalar(minus_bias[:, k * NT0:(k + 1) * NT0], v(bias, 0, NT0), v(sub), None, ALU.mult).then_inc(w0_lo, 1)
            for s in bank_taken:
                dve.sem_inc(s, 1)
            with dve.Fori(0, LOOPS) as loop:
                def full_tile(step, k=0):
                    s = banks.slot(step, k)
                    dve.wait_ge(bank_full[s], banks.nth(loop, step, k))
                    return bank[s], bank_taken[s]

                def taken_tile(step, k=0):
                    s = banks.slot(step, k)
                    dve.wait_ge(bank_taken[s], banks.taken(loop, step, k))

                def low_part(step, n, k=0, bias=None, at=0):
                    j = step[2]
                    ps, taken = full_tile(step, k)
                    dve.wait_ge(hi_set, hi_n.at(loop, step, k + 1))
                    hi = qkh[j][:, at:at + n].bitcast(F32)
                    if bias is None:
                        dve.tensor_tensor(qkl[j][:, at:at + n], ps[:, 0:n], hi, ALU.subtract).then_inc(taken, 1)
                    else:
                        dve.scalar_tensor_tensor(qkl[j][:, at:at + n], ps[:, 0:n], bias, hi, ALU.add, ALU.subtract).then_inc(taken, 1)

                for step in SCHEDULE:
                    kind, phase, j, i = step
                    if kind == "ln":
                        if phase == "sa0":
                            dve.wait_ge(x_loaded[j], loop * 16 + 16)
                        else:
                            taken_tile(("yT", PHASES[PHASES.index(phase) - 1], j, 0))
                        if phase == "ca1":
                            dve.sem_inc(x_used[j], 1)
                        elif phase == "ff1":
                            dve.sem_inc(ctx_used[j], 1)
                        src = tokens(j, phase)
                        for t in range(QT):
                            dve.bn_stats(stats[j][:, t, :], src[:, t, :]).then_inc(ln_step, 1)
                        dve.wait_ge(ln_step, ln_n.at(loop, step, 2))
                        dve.sem_inc(dve_passed, 1)
                        for t in range(QT):
                            dve.bn_aggr(mv[j][:, t, :], stats[j][:, t, :]).then_inc(ln_step, 1)
                        dve.wait_ge(ln_step, ln_n.at(loop, step, 4))
                        dve.tensor_scalar(ve[j][:], mv[j][:, :, 1], EPS, None, ALU.add).then_inc(ln_step, 1)
                    elif kind == "nm":
                        src = tokens(j, phase)
                        dve.wait_ge(rstd_set, rstd_n.at(loop, ("ln", phase, j, 0)))
                        for t in range(QT):
                            dve.tensor_scalar(yT[j][:, t * P:(t + 1) * P], src[:, t, :], mv[j][:, t, 0:1], rstd[j][:, t:t + 1],
                                              ALU.subtract, ALU.mult).then_inc(ln_step, 1)
                    elif kind == "hT":
                        taken_tile(step)
                        if phase == "ca0":
                            dve.wait_ge(pool_set, pool_n.at(loop, ("ck0", phase, j, 0)))
                            dve.sem_inc(dve_passed, 1)
                        dve.tensor_copy(hh[j][:], yT[j][:]).then_inc(h_split, 1)
                        dve.wait_ge(h_split, h_n.at(loop, step, 1))
                        dve.tensor_tensor(hl[j][:], yT[j][:], hh[j][:].bitcast(F32), ALU.subtract).then_inc(h_split, 1)
                    elif kind == "qk0":
                        for k in range(4):
                            ps, taken = full_tile(step, k)
                            dve.wait_ge(hi_set, hi_n.at(loop, step, k + 1))
                            for t in range(2):
                                n = 2 * (k % 2) + t
                                at = k * BANK + t * TOK
                                ins = dve.scalar_tensor_tensor((qs if k < 2 else ks)(j)[:, n, :], ps[:, t * TOK:(t + 1) * TOK], v("bqs" if k < 2 else "bks", n),
                                                               qkl[j][:, at:at + TOK].bitcast(F32), ALU.add, ALU.add)
                            ins.then_inc(taken, 1)
                    elif kind == "v0":
                        dve.wait_ge(pool_set, pool_n.at(loop, step))
                        ps, taken = full_tile(step)
                        dve.tensor_tensor(v32(j)[:, :, :, 0:HD0], ps[:, 0:TOK].rearrange("p (t h d) -> p t h d", t=QT, h=H),
                                          bv[:, 0, :].rearrange("p (h d) -> p h d", h=H).unsqueeze(1).broadcast_to([P, QT, H, HD0]),
                                          ALU.add).then_inc(taken, 1)
                    elif kind in ("b0", "b1"):
                        if kind == "b0":
                            dve.wait_ge(pool_set, pool_n.at(loop, ("qk0", phase, j, 0)))
                        for g in range(2):
                            ps, taken = full_tile(step, g)
                            if kind == "b0":
                                dst = mx0(j)[:, :, i // 2, 32 * (2 * (i % 2) + g) + 24]
                            else:
                                dst = raw_max(j)[:, :, g, i]
                            dve.tensor_reduce(dst, ps[:].rearrange("p (q k) -> p q k", q=QT), AX_X, ALU.max, negate=True).then_inc(taken, 1)
                    elif kind == "bc":
                        for k in range(2):
                            ps, taken = full_tile(step, k)
                            dst = raw_max(j)[:, i, :, 4 * k:4 * k + 4].rearrange("p g w -> p w g")
                            dve.tensor_reduce(dst, ps[:].rearrange("p (w g k) -> p w g k", g=2, k=KEYS), AX_X, ALU.max,
                                              negate=True).then_inc(taken, 1)
                    elif kind == "mc":
                        dve.wait_ge(pool_set, pool_n.at(loop, ("hT", phase, j, 0)))
                        taken_tile(("b1", phase, j, HP - 1) if phase == "sa1" else ("bc", phase, j, 1), 1)
                        hi, lo = (mxc(j).rearrange("p q (g c) -> p q g c", g=2)[:, :, :, a:a + HP] for a in (0, HP))
                        dve.tensor_copy(hi, raw_max(j)).then_inc(max_set, 1)
                        dve.wait_ge(max_set, max_n.at(loop, step, 1))
                        dve.tensor_tensor(lo, raw_max(j), hi, ALU.subtract).then_inc(max_set, 1)
                    elif kind == "m0":
                        for k in range(2):
                            ps, taken = full_tile(step, k)
                            cols = slice(k * BANK, (k + 1) * BANK)
                            dve.tensor_tensor(qm(j).rearrange("p t q -> p (t q)")[:, cols], qs(j).rearrange("p t q -> p (t q)")[:, cols].bitcast(F32),
                                              ps[:], ALU.add).then_inc(taken, 1)
                    elif kind == "o0":
                        for k in range(QT):
                            ps, taken = full_tile(step, k)
                            o = ps[:].rearrange("p (h c) -> p h c", h=H)
                            den = rden[j][:, k * H:(k + 1) * H]
                            dve.reciprocal(den, o[:, :, HD0]).then_inc(norm_step, 1)
                            dve.wait_ge(norm_step, norm_n.at(loop, step, k + 1))
                            dve.tensor_tensor(on[j][:, k * P:(k + 1) * P].rearrange("p (h d) -> p h d", h=H), o[:, :, 0:HD0],
                                              spread(den, HD0), ALU.mult).then_inc(taken, 1)
                    elif kind in ("pv1", "pvc1"):
                        ps, taken = full_tile(step)
                        order = "p (g t c) -> p g t c" if kind == "pv1" else "p (t g c) -> p g t c"
                        o = ps[:, 0:4 * 65].rearrange(order, g=2, t=QT)
                        den = rden[j][:, 4 * i:4 * i + 4].rearrange("p (g t) -> p g t", g=2)
                        dve.reciprocal(den, o[:, :, :, HD1]).then_inc(norm_step, 1)
                        dve.wait_ge(norm_step, norm_n.at(loop, step))
                        dst = on[j][:].rearrange("p (t h d) -> p h t d", t=QT, h=H)[:, 2 * i:2 * i + 2]
                        dve.tensor_tensor(dst, o[:, :, :, 0:HD1], spread(den, HD1), ALU.mult).then_inc(taken, 1)
                    elif kind == "oT":
                        low_part(step, TOK)
                    elif kind == "q0c":
                        low_part(step, TOK, bias=v("cbq"))
                    elif kind in ("qk1", "o1"):
                        low_part(step, BANK, at=i * BANK)
                    elif kind == "g1":
                        for k in range(2):
                            low_part(step, BANK, k=k, at=2048 + k * BANK)
                    elif kind == "yT":
                        ps, taken = full_tile(step)
                        if phase == "sa0":
                            dve.wait_ge(stored[j], loop * 16 + 16)
                        dve.tensor_tensor(x[j][:].rearrange("p t d -> p (t d)"), tokens(j, phase)[:, :, :].rearrange("p t d -> p (t d)"), ps[:, 0:TOK],
                                          ALU.add).then_inc(taken, 1)
                    elif kind == "ck0":
                        ps, taken = full_tile(step)
                        dve.tensor_scalar(yT[j][:, 0:KEYS], ps[:, 0:KEYS], v("cbk"), None, ALU.add).then_inc(kc_step, 1)
                        dve.wait_ge(kc_step, kc_n.at(loop, step, 1))
                        dve.tensor_copy(hh[j][:, 0:KEYS], yT[j][:, 0:KEYS]).then_inc(kc_step, 1)
                        dve.wait_ge(kc_step, kc_n.at(loop, step, 2))
                        dve.tensor_tensor(hl[j][:, 0:KEYS], yT[j][:, 0:KEYS], hh[j][:, 0:KEYS].bitcast(F32), ALU.subtract).then_inc(kc_step, 1)
                        dve.wait_ge(pool_set, pool_n.at(loop, step, 3))
                        val = ps[:, KEYS:KEYS + D].rearrange("p (w g d) -> p w g d", g=2, d=HD0)
                        bias = bv[:, 1, :].rearrange("p (w g d) -> p w g d", g=2, d=HD0)
                        dve.tensor_tensor(vb0(j)[0:KEYS, :, 0:HD0], val[0:KEYS, :, 0, :], bias[0:KEYS, :, 0, :], ALU.add).then_inc(kc_step, 1)
                        dve.tensor_tensor(vb0(j)[KEYS:P, :, 32:32 + HD0], val[KEYS:P, :, 1, :], bias[KEYS:P, :, 1, :], ALU.add).then_inc(taken, 1)
                    elif kind == "w1":
                        for k in range(2):
                            taken_tile(step, k)
                            cols = slice(k * BANK, (k + 1) * BANK)
                            dve.tensor_copy(qkh[j][:, cols], on[j][:, cols]).then_inc(g_step, 1)
                            dve.wait_ge(g_step, g_n.at(loop, step, 2 * k + 1))
                            dve.tensor_tensor(qkl[j][:, cols], on[j][:, cols], qkh[j][:, cols].bitcast(F32), ALU.subtract).then_inc(g_step, 1)
                    elif kind == "wp":
                        ps, taken = full_tile(step)
                        dve.wait_ge(hi_set, hi_n.at(loop, step))
                        cols = slice(i * TOK, (i + 1) * TOK)
                        dve.scalar_tensor_tensor(on[j][:, cols], ps[:, 0:TOK], v("bp", i), on[j][:, 1024 + i * TOK:1024 + (i + 1) * TOK],
                                                 ALU.add, ALU.mult).then_inc(taken, 1)
                        taken_tile(step)
                        dve.tensor_copy(qkh[j][:, cols], on[j][:, cols]).then_inc(g_step, 1)
                        dve.wait_ge(g_step, g_n.at(loop, step, 1))
                        dve.tensor_tensor(qkl[j][:, cols], on[j][:, cols], qkh[j][:, cols].bitcast(F32), ALU.subtract).then_inc(g_step, 1)

        @block.tensor
        def _(pe):
            pe.wait_ge(w0_hi, 2)
            pe.wait_ge(w0_lo, 2)
            pe.wait_ge(small_loaded, 64)
            pe.wait_ge(wn_loaded, 32)
            pe.wait_ge(w1_hi, 4)
            pe.wait_ge(w1_lo, 4)

            def three(dst, a, b, start=True, stop=True):
                passes = ((0, 0), (0, 1), (1, 0))
                for n, (p, q) in enumerate(passes):
                    ins = pe.matmul(dst, a[p], b[q], start=start and n == 0, stop=stop and n == 2)
                return ins

            with pe.Fori(0, LOOPS) as loop:
                def free_tiles(step, *own, after=()):
                    need = {}
                    for use in (*after, *[(step, k) for k in own]):
                        slot, n = banks.use[use]
                        need[slot] = max(need.get(slot, 0), n if use[0] == step else n + 1)
                    for slot, n in need.items():
                        pe.wait_ge(bank_taken[slot], loop * banks.per_slot[slot] + n)
                    return [(bank[banks.slot(step, k)], bank_full[banks.slot(step, k)]) for k in own]

                def free_tile(step, k=0, after=()):
                    return free_tiles(step, k, after=after)[0]

                for step in SCHEDULE:
                    kind, phase, j, i = step
                    if kind == "hT":
                        pe.wait_ge(ln_step, ln_n.at(loop, ("nm", phase, j, 0)))
                        ps, full = free_tile(step)
                        for t in range(QT):
                            ins = pe.transpose(ps[:, t * P:(t + 1) * P], yT[j][:, t * P:(t + 1) * P], ident[:])
                        ins.then_inc(full, 1)
                    elif kind == "qk0":
                        pe.wait_ge(h_split, h_n.at(loop, ("hT", phase, j, 0)))
                        for k in range(4):
                            ps, full = free_tile(step, k)
                            for t in range(2):
                                a = P * (2 * (k % 2) + t)
                                wide = [w(n, "wq0" if k < 2 else "wk0", a, a + P) for n in range(2)]
                                ins = three(ps[:, t * TOK:(t + 1) * TOK], wide, (hh[j][:], hl[j][:]))
                            ins.then_inc(full, 1)
                    elif kind == "v0":
                        pe.wait_ge(h_split, h_n.at(loop, ("hT", phase, j, 0)))
                        ps, full = free_tile(step)
                        for t in range(QT):
                            a = slice(t * P, (t + 1) * P)
                            ins = three(ps[:, a], (hh[j][:, a], hl[j][:, a]), (w(0, "wv0", 0, D), w(1, "wv0", 0, D)))
                        ins.then_inc(full, 1)
                    elif kind == "b0":
                        two = free_tiles(step, 0, 1, after=[(("qk0", phase, j, 0), k) for k in range(4)] if i == 0 else ())
                        t = i // 2
                        for q in range(QT):
                            for g, (ps, full) in enumerate(two):
                                r = slice(32 * (2 * (i % 2) + g), 32 * (2 * (i % 2) + g) + 32)
                                ins = pe.matmul(ps[:, q * TOK:(q + 1) * TOK], qs(j)[r, t, q * P:(q + 1) * P], ks(j)[r, t, :],
                                                start=True, stop=True, tile_position=(r.start, 0))
                                if q == QT - 1:
                                    ins.then_inc(full, 1)
                    elif kind == "m0":
                        for k in range(2):
                            ps, full = free_tile(step, k, after=[(("b0", phase, j, 7), 1)])
                            for t in range(2):
                                for q in range(QT):
                                    a = (t * QT + q) * P
                                    ins = pe.transpose(ps[:, a:a + P], mx0(j)[:, q, 2 * k + t, :], ident[:])
                            ins.then_inc(full, 1)
                    elif kind == "c0":
                        two = free_tiles(step, 0, 1, after=[(("m0", phase, j, 0), k) for k in range(2)] if i == 0 else ())
                        t = i // 2
                        for q in range(QT):
                            for g, (ps, full) in enumerate(two):
                                r = slice(32 * (2 * (i % 2) + g), 32 * (2 * (i % 2) + g) + 32)
                                ins = pe.matmul(ps[:, q * TOK:(q + 1) * TOK], ks(j)[r, t, q * P:(q + 1) * P], qm(j)[r, t, :],
                                                start=True, stop=True, tile_position=(r.start, 0))
                                if q == QT - 1:
                                    ins.then_inc(full, 1)
                    elif kind == "pv0":
                        after = [(("c0", phase, j, 2 * i + 1), 1)]
                        if i == 0:
                            after.append((("v0", phase, j, 0), 0))
                        use = ("pv0", phase, j, i - i % 2)
                        if i % 2 == 0:
                            ps, full = free_tile(step, after=after)
                        else:
                            free_tiles(step, after=after)
                            ps, full = bank[banks.slot(use)], bank_full[banks.slot(use)]
                        for k in range(QT):
                            for g in range(4):
                                e = slot_of[("c0", phase, j, 2 * i + g // 2)]
                                a = ((g % 2) * QT + k) * TOK
                                ins = pe.matmul(ps[32 * g:32 * g + 32, (i % 2) * TOK:(i % 2 + 1) * TOK], v32(j)[:, k, 4 * i + g, :],
                                                probs[:, e, a:a + TOK], start=k == 0, stop=k == QT - 1, tile_position=(0, 32 * g))
                        if i % 2:
                            ins.then_inc(full, 1)
                    elif kind == "o0":
                        after = [(("pv0", phase, j, 2) if phase == "sa0" else ("pvc0", phase, j, 1), 0)]
                        for q in range(QT):
                            ps, full = free_tile(step, q, after=after)
                            for t in range(NT0):
                                ins = pe.transpose(ps[:, t * P:(t + 1) * P], oT0(j)[:, t * TOK + q * P:t * TOK + (q + 1) * P], ident[:])
                            ins.then_inc(full, 1)
                    elif kind == "oT":
                        ps, full = free_tile(step, after=[(("o0", phase, j, 0), k) for k in range(QT)])
                        for q in range(QT):
                            ins = pe.transpose(ps[:, q * P:(q + 1) * P], on[j][:, q * P:(q + 1) * P], ident[:])
                        ins.then_inc(full, 1)
                    elif kind == "wo":
                        after = []
                        if phase in ("sa0", "ca0"):
                            after = [(("oT", phase, j, 0), 0)]
                            name, n = ("wo0" if phase == "sa0" else "cwo0"), 1
                        elif phase in ("sa1", "ca1"):
                            after = [(("o1", phase, j, k), 0) for k in range(4)]
                            name, n = ("wo1" if phase == "sa1" else "wo2"), HP
                        else:
                            pe.wait_ge(g_step, g_n.at(loop, ("w1", phase, j, 0) if phase == "ff0" else ("wp", phase, j, 3)))
                            name, n = ("w2" if phase == "ff0" else "wf"), FF // P
                        ps, full = free_tile(step, after=after)
                        for k in range(n):
                            b = slice(k * TOK, (k + 1) * TOK)
                            ins = three(ps[:, 0:TOK], [w(m, name, k * P, (k + 1) * P) for m in range(2)], (qkh[j][:, b], qkl[j][:, b]),
                                        start=k == 0, stop=k == n - 1)
                        ins.then_inc(full, 1)
                    elif kind == "yT":
                        ps, full = free_tile(step, after=[(("wo", phase, j, 0), 0)])
                        for q in range(QT):
                            ins = pe.transpose(ps[:, q * P:(q + 1) * P], yT[j][:, q * P:(q + 1) * P], ident[:])
                        ins.then_inc(full, 1)
                    elif kind == "ck0":
                        pe.wait_ge(ctx_loaded[j], loop * 32 + 32)
                        ps, full = free_tile(step)
                        pe.matmul(ps[:, 0:KEYS], kv0[:, 0:D], ct[j][:, 0, :], start=True, stop=True)
                        pe.matmul(ps[:, KEYS:KEYS + D], ct[j][:].rearrange("c a k -> c (a k)"), kv0[:, D:2 * D],
                                  start=True, stop=True).then_inc(full, 1)
                    elif kind == "q0c":
                        pe.wait_ge(h_split, h_n.at(loop, ("hT", phase, j, 0)))
                        ps, full = free_tile(step)
                        three(ps[:, 0:TOK], [w(m, "cwq0", 0, D) for m in range(2)], (hh[j][:], hl[j][:])).then_inc(full, 1)
                    elif kind == "bc":
                        if phase == "ca0":
                            after = [(("q0c", phase, j, 0), 0)]
                            pe.wait_ge(pool_set, pool_n.at(loop, ("ck0", phase, j, 0)))
                        else:
                            after = [(("g1", phase, j, 0), k) for k in range(2)]
                            pe.wait_ge(h_split, h_n.at(loop, ("hT", phase, j, 0)))
                        two = free_tiles(step, 0, 1, after=after)
                        q_hi = crossq(j, phase)[0]
                        for n, (ps, full) in enumerate(two):
                            ins = pe.matmul(ps[:], q_hi[:, i * P:(i + 1) * P], g_of(qkh, j)[:, n * BANK:(n + 1) * BANK],
                                            start=True, stop=True)
                            ins.then_inc(full, 1)
                    elif kind == "mc":
                        pe.wait_ge(max_set, max_n.at(loop, step))
                        ps, full = free_tile(step)
                        for q in range(QT):
                            ins = pe.transpose(ps[:, 0:P].bitcast(BF16)[:, q * P:(q + 1) * P], mxc(j)[:, q, :], identb[:])
                        ins.then_inc(full, 1)
                    elif kind == "cc":
                        two = free_tiles(step, 0, 1, after=[(("mc", phase, j, 0), 0)])
                        for n in range(4):
                            pair = 4 * i + n
                            ps, full = two[n // 2]
                            dst = ps[:, (n % 2) * TOK:(n % 2 + 1) * TOK]
                            a = slice(pair * P, (pair + 1) * P)
                            qh_, ql_ = crossq(j, phase)
                            three(dst, (g_of(qkh, j)[:, a], g_of(qkl, j)[:, a]), (qh_[:, 0:TOK], ql_[:, 0:TOK]), stop=False)
                            ins = pe.matmul(dst, select[:, a], aug[j][:], start=False, stop=True)
                            if n % 2:
                                ins.then_inc(full, 1)
                    elif kind == "pvc0":
                        e = ("cc", phase, j, i)
                        after = [(e, 1)]
                        if i == 0:
                            after.append((("ck0", phase, j, 0), 0))
                        ps, full = free_tile(step, after=after)
                        for n in range(4):
                            r = 64 * (n % 2)
                            ins = pe.matmul(ps[r:r + 64, (n // 2) * TOK:(n // 2 + 1) * TOK], vb0(j)[:, 4 * i + n, :],
                                            probs[:, slot_of[e], n * TOK:(n + 1) * TOK], start=True, stop=True, tile_position=(0, r))
                        ins.then_inc(full, 1)
                    elif kind == "w1":
                        pe.wait_ge(h_split, h_n.at(loop, ("hT", phase, j, 0)))
                        for k in range(2):
                            ps, full = free_tile(step, k)
                            for t in range(2):
                                a = (2 * k + t) * P
                                ins = three(ps[:, t * TOK:(t + 1) * TOK], [w(m, "w1", a, a + P) for m in range(2)], (hh[j][:], hl[j][:]))
                            ins.then_inc(full, 1)
                    elif kind == "qk1":
                        pe.wait_ge(h_split, h_n.at(loop, ("hT", phase, j, 0)))
                        ps, full = free_tile(step)
                        for t, name in enumerate(("wq1", "wk1")):
                            ins = three(ps[:, t * TOK:(t + 1) * TOK], [w(m, name, i * P, (i + 1) * P) for m in range(2)], (hh[j][:], hl[j][:]))
                        ins.then_inc(full, 1)
                    elif kind == "v1":
                        pe.wait_ge(h_split, h_n.at(loop, ("hT", phase, j, 0)))
                        ps, full = free_tile(step)
                        t, half = divmod(i, 2)
                        a = slice(t * P, (t + 1) * P)
                        three(ps[:], (hh[j][:, a], hl[j][:, a]), [w(m, "wv1", half * BANK, (half + 1) * BANK) for m in range(2)]).then_inc(full, 1)
                    elif kind == "b1":
                        two = free_tiles(step, 0, 1, after=[(("qk1", phase, j, i), 0)])
                        for q in range(QT):
                            for g, (ps, full) in enumerate(two):
                                r = slice(64 * g, 64 * g + 64)
                                ins = pe.matmul(ps[:, q * TOK:(q + 1) * TOK], qk(qkh, j, i, 0)[r, q * P:(q + 1) * P], qk(qkh, j, i, 1)[r, :],
                                                start=True, stop=True)
                                if q == QT - 1:
                                    ins.then_inc(full, 1)
                    elif kind == "c1":
                        two = free_tiles(step, 0, 1, after=[(("mc", phase, j, 0), 0)])
                        for t in range(QT):
                            keys = slice(t * P, (t + 1) * P)
                            for n, (kp, qp) in enumerate(((qkh, qkh), (qkh, qkl), (qkl, qkh))):
                                for g, (ps, _) in enumerate(two):
                                    r = slice(64 * g, 64 * g + 64)
                                    pe.matmul(ps[:, t * TOK:(t + 1) * TOK], qk(kp, j, i, 1)[r, keys], qk(qp, j, i, 0)[r, :],
                                              start=n == 0, stop=False)
                            for g, (ps, full) in enumerate(two):
                                ins = pe.matmul(ps[:, t * TOK:(t + 1) * TOK], select[:, i * P + 64 * g:i * P + 64 * g + 1].broadcast_to([P, P]),
                                                aug[j][:], start=False, stop=True)
                                if t == QT - 1:
                                    ins.then_inc(full, 1)
                    elif kind == "pv1":
                        e = ("c1", phase, j, i)
                        after = [(e, 1)]
                        if i == 0:
                            pe.wait_ge(pool_set, pool_n.at(loop, ("v1", phase, j, 0)))
                            after.append((("v1", phase, j, 3), 0))
                        ps, full = free_tile(step, after=after)
                        for g in range(2):
                            for q in range(QT):
                                for k in range(QT):
                                    a = (g * QT + k) * TOK + q * P
                                    ins = pe.matmul(ps[:, (g * QT + q) * 65:(g * QT + q + 1) * 65], probs[:, slot_of[e], a:a + P],
                                                    v65(j)[:, k, 2 * i + g, :], start=k == 0, stop=k == QT - 1)
                        ins.then_inc(full, 1)
                    elif kind == "pvc1":
                        e = ("cc", phase, j, i // 4)
                        after = [(e, 1)] if i % 4 == 0 else []
                        if i == 0:
                            after.append((("cv1", phase, j, 0), 1))
                        ps, full = free_tile(step, after=after)
                        for q in range(QT):
                            a = (i % 4) * TOK + q * P
                            ins = pe.matmul(ps[:, q * 130:(q + 1) * 130], probs[:, slot_of[e], a:a + P], vb1(j)[:, i, :], start=True, stop=True)
                        ins.then_inc(full, 1)
                    elif kind == "o1":
                        after = [(("pv1" if phase == "sa1" else "pvc1", phase, j, HP - 1), 0)] if i == 0 else ()
                        ps, full = free_tile(step, after=after)
                        for t in range(2):
                            for q in range(QT):
                                a, b = q * 1024 + (2 * i + t) * P, (t * QT + q) * P
                                ins = pe.transpose(ps[:, b:b + P], on[j][:, a:a + P], ident[:])
                        ins.then_inc(full, 1)
                    elif kind == "ck1":
                        ps, full = free_tile(step)
                        for k in range(HP):
                            ins = pe.matmul(ps[:, k * KEYS:(k + 1) * KEYS], kv1[0:CTX, 0, k * P:(k + 1) * P], ct[j][:, 0, :], start=True, stop=True)
                        ins.then_inc(full, 1)
                    elif kind == "g1":
                        for k in range(2):
                            ps, full = free_tile(step, k, after=[(("ck1", phase, j, 0), 0)])
                            for n in range(4):
                                a = slice((4 * k + n) * P, (4 * k + n + 1) * P)
                                ins = pe.matmul(ps[:, n * P:(n + 1) * P], kv1[:, 2, a], on[j][:, a], start=True, stop=True)
                            ins.then_inc(full, 1)
                    elif kind == "cv1":
                        for k in range(2):
                            ps, full = free_tile(step, k)
                            pe.matmul(ps[:], ct[j][:].rearrange("c a k -> c (a k)"), kv1[0:CTX, 1, k * BANK:(k + 1) * BANK],
                                      start=True, stop=True).then_inc(full, 1)
                    elif kind == "wp":
                        pe.wait_ge(h_split, h_n.at(loop, ("hT", phase, j, 0)))
                        ps, full = free_tile(step)
                        for t in range(2):
                            a = t * FF + i * P
                            ins = three(ps[:, t * TOK:(t + 1) * TOK], [w(m, "wp", a, a + P) for m in range(2)], (hh[j][:], hl[j][:]))
                        ins.then_inc(full, 1)


def kernel(**inputs):
    import concourse.bacc as bacc
    from concourse.bass_utils import run_bass_kernel_spmd

    a = {k: np.asarray(t) for k, t in inputs.items()}

    def turned(name):
        return np.ascontiguousarray(a[name].T)

    def by_rows(m):
        n = m.shape[0] // P
        return m.reshape(n, P, -1).transpose(1, 0, 2).reshape(P, -1)

    def three_times(m):
        m = m.reshape(P, H, 1, HD0)
        return np.concatenate([m, m, m, np.zeros_like(m)], axis=2).reshape(P, 4 * P)

    w0 = np.concatenate([three_times(turned("L0_xattn_sa_wq")), three_times(turned("L0_xattn_sa_wk")), turned("L0_xattn_sa_wv"), turned("L0_xattn_sa_wo"),
                         turned("L0_xattn_ca_wq"), turned("L0_xattn_ca_wo"), turned("L0_xattn_mlp_w1"),
                         by_rows(turned("L0_xattn_mlp_w2"))], axis=1)
    w1 = np.concatenate([a["L1_xattn_Wq1"], a["L1_xattn_Wk1"], a["L1_xattn_Wv1"], by_rows(a["L1_xattn_Wo1"]), by_rows(a["L1_xattn_Wo2"]),
                         a["L1_xattn_Wp"], by_rows(a["L1_xattn_Wf"])], axis=1)
    kv0 = np.concatenate([turned("L0_xattn_ca_wk"), turned("L0_xattn_ca_wv")], axis=1)
    kv1 = np.zeros((P, 3, 1024), np.float32)
    kv1[:CTX, 0], kv1[:CTX, 1], kv1[:, 2] = a["L1_xattn_Wk2"], a["L1_xattn_Wv2"], by_rows(turned("L1_xattn_Wq2"))

    def stacked(bias, one):
        b = bias.reshape(NT0, 4, 1, HD0)
        rest = np.zeros((NT0, 4, 1, HD0), np.float32)
        rest[..., 0] = one
        return np.concatenate([b, b, b, rest], axis=2).reshape(NT0, P).T

    row = np.arange(P)
    part = (row % 32) // HD0
    cols = lambda name: a[name].reshape(-1, P).T
    vec = {"bqs": stacked(a["L0_xattn_sa_bq"], 0), "bks": stacked(a["L0_xattn_sa_bk"], 1),
           "cbq": cols("L0_xattn_ca_bq"), "cbk": cols("L0_xattn_ca_bk"), "bo0": cols("L0_xattn_sa_bo"), "cbo0": cols("L0_xattn_ca_bo"),
           "b1m": cols("L0_xattn_mlp_b1"), "b2m": cols("L0_xattn_mlp_b2"), "bo1": cols("L1_xattn_bo1"), "bo2": cols("L1_xattn_bo2"),
           "bp": cols("L1_xattn_bp"), "bf": cols("L1_xattn_bf"),
           "subq": -(part == 1).astype(np.float32)[:, None],
           "subk": -(part == 2).astype(np.float32)[:, None],
           "mask": (row[:, None] // HD0 == np.arange(H)).astype(np.float32), "half": np.full((P, QT), -0.5, np.float32)}
    for n, (g, b) in enumerate([(f"L{l}_xattn_{g}{k}{e}", f"L{l}_xattn_{b}{k}{f}") for l, g, b, e, f in ((0, "ln", "ln", "_g", "_b"), (1, "g", "b", "", ""))
                                for k in (1, 2, 3)]):
        vec[f"g{n}"], vec[f"b{n}"] = cols(g), cols(b)
    vec = np.ascontiguousarray(np.concatenate([vec[name] for name in VEC_NAMES], axis=1))
    assert vec.shape[1] == VEC_N and w0.shape[1] == W0_N and w1.shape[1] == W1_N
    pair, col = np.arange(HP * P) // P, np.arange(HP * P) % P
    r = row[:, None]
    select = ((r // 64 == col // 64) & (r % 64 < 2 * HP) & (r % HP == pair)).astype(np.float32)
    arrays = {"x_in": a["x"], "ctx_in": np.ascontiguousarray(a["ctx_768"].transpose(0, 2, 1)), "w0_in": np.ascontiguousarray(w0), "w1_in": np.ascontiguousarray(w1),
              "kv0_in": np.ascontiguousarray(kv0), "kv1_in": kv1.reshape(P, -1), "vec_in": vec,
              "bv_in": np.concatenate([a["L0_xattn_sa_bv"], a["L0_xattn_ca_bv"]]), "id_in": np.eye(P, dtype=np.float32), "sel_in": select}
    nc = bacc.Bacc("TRN2", target_bir_lowering=False, num_devices=1)
    args = [nc.dram_tensor(k, t.shape, F32, kind="ExternalInput").ap() for k, t in arrays.items()]
    out = nc.dram_tensor("out", (BATCH, TOK, D), F32, kind="ExternalOutput").ap()
    build(nc, *args, out)
    r = run_bass_kernel_spmd(nc, [arrays], core_ids=[0])
    return r.results[0]["out"]
```
